# Optimizing a Trainium2 kernel written in Bass

```python
import numpy as np
import jax
import jax.numpy as jnp

def _softmax(x, axis=-1):
    return jax.nn.softmax(x, axis=axis)

def _gelu(x):
    return jax.nn.gelu(x, approximate=True)

def _silu(x):
    return jax.nn.silu(x)

def _sigmoid(x):
    return jax.nn.sigmoid(x)

def _layernorm(x, axis=-1, eps=1e-05):
    m = jnp.mean(x, axis=axis, keepdims=True)
    v = jnp.var(x, axis=axis, keepdims=True)
    return (x - m) / jnp.sqrt(v + eps)

def _scatter_add(tgt, idx, src, axis=0):
    return tgt.at[idx].add(src)

def _segment_sum(src, seg, n):
    return jax.ops.segment_sum(src, seg, n)
kernel_name = 'mk_gnn_resnorm_d2_gnn_r32_ec2ac8'

def setup_inputs(seed: int=0):
    np.random.seed(seed)
    _w = jnp.asarray

    def _rec_inputs():
        import jax
        import jax.numpy as jnp
        _gk = jax.random.key(seed)
        x = -8.776e-05 + 1 * jax.random.normal(jax.random.fold_in(_gk, 1), (50000, 256), jnp.float32)
        src = jax.random.randint(jax.random.fold_in(_gk, 2), (50000,), 0, 50000, jnp.int32)
        dst = jax.random.randint(jax.random.fold_in(_gk, 3), (50000,), 0, 50000, jnp.int32)
        _o = jnp.argsort(dst, stable=True)
        src = src[_o]
        dst = dst[_o]
        edge_attr_128 = -1.52775e-05 + 0.999936 * jax.random.normal(jax.random.fold_in(_gk, 12), (50000, 128), jnp.float32)
        edge_attr_32 = 0.000268479 + 0.999861 * jax.random.normal(jax.random.fold_in(_gk, 13), (50000, 32), jnp.float32)
        return (x, src, dst, edge_attr_128, edge_attr_32)
    x, src, dst, edge_attr_128, edge_attr_32 = _rec_inputs()

    def _L0_gnn_setup():
        import jax, jax.numpy as jnp
        import numpy as np
        N = 625
        E = 10000
        IN_DIM = 256
        OUT_DIM = 64
        HEADS = 4
        EDGE_DIM = 32
        NEG_SLOPE = 0.2

        def _gat_forward(x, edge_attr, lin_W, att_src, att_dst, lin_edge_W, att_edge, bias, edge_index):
            n = x.shape[0]
            loops = jnp.arange(n, dtype=edge_index.dtype)
            ei = jnp.concatenate([edge_index, jnp.stack([loops, loops])], axis=1)
            ea = jnp.concatenate([edge_attr, jnp.zeros((n, edge_attr.shape[1]), edge_attr.dtype)], axis=0)
            src, dst = (ei[0], ei[1])
            x_proj = (x @ lin_W.T).reshape(n, HEADS, OUT_DIM)
            s_src = jnp.einsum('nhd,hd->nh', x_proj, att_src)
            s_dst = jnp.einsum('nhd,hd->nh', x_proj, att_dst)
            att = s_src[src] + s_dst[dst]
            e_proj = (ea @ lin_edge_W.T).reshape(-1, HEADS, OUT_DIM)
            att = att + jnp.einsum('ehd,hd->eh', e_proj, att_edge)
            att = jnp.where(att >= 0, att, NEG_SLOPE * att)
            seg_max = jax.ops.segment_max(att, dst, num_segments=n)
            exps = jnp.exp(att - seg_max[dst])
            denom = jax.ops.segment_sum(exps, dst, num_segments=n)
            alpha = exps / (denom[dst] + 1e-12)
            m = x_proj[src] * alpha[:, :, None]
            out = jax.ops.segment_sum(m, dst, num_segments=n)
            out = out.reshape(n, HEADS * OUT_DIM) + bias
            return out
        key = jax.random.key(seed)
        ks = jax.random.split(key, 10)
        HD = HEADS * OUT_DIM
        x = jax.random.normal(ks[0], (N, IN_DIM), dtype=jnp.float32)
        edge_index = jax.random.randint(ks[1], (2, E), 0, N, dtype=jnp.int64)
        edge_attr = jax.random.normal(ks[2], (E, EDGE_DIM), dtype=jnp.float32)

        def xavier(k, shape):
            fan_in, fan_out = (shape[1], shape[0])
            a = np.sqrt(2.0) * np.sqrt(6.0 / (fan_in + fan_out))
            return jax.random.uniform(k, shape, jnp.float32, -a, a)
        lin_W = xavier(ks[3], (HD, IN_DIM))
        att_src = xavier(ks[4], (HEADS, OUT_DIM))
        att_dst = xavier(ks[5], (HEADS, OUT_DIM))
        lin_edge_W = xavier(ks[6], (HD, EDGE_DIM))
        att_edge = xavier(ks[7], (HEADS, OUT_DIM))
        bias = jnp.zeros((HD,), dtype=jnp.float32)
        return {'x': x, 'edge_index': edge_index, 'edge_attr': edge_attr, 'lin_W': lin_W, 'att_src': att_src, 'att_dst': att_dst, 'lin_edge_W': lin_edge_W, 'att_edge': att_edge, 'bias': bias}
    _L0_gnn_all = _L0_gnn_setup()
    _L0_gnn_in = {k: v for k, v in _L0_gnn_all.items() if k in ('lin_W', 'att_src', 'att_dst', 'lin_edge_W', 'att_edge', 'bias')}
    del _L0_gnn_all

    def _L1_gnn_setup():
        import jax, jax.numpy as jnp
        import numpy as np
        N_NODES = 512
        N_EDGES = 8192
        D_NODE = 256
        D_EDGE = 128
        OUT_DIM = 256
        N_LAYERS = 3

        def _auto_mlp_dims(inp_dim, out_dim, n_layers):
            dims = np.logspace(np.log(inp_dim), np.log(out_dim), n_layers + 1, base=np.e)
            return [int(d) for d in np.round(dims)[1:]]

        def _segment_mean(data, seg, num_segments):
            s = jax.ops.segment_sum(data, seg, num_segments=num_segments, indices_are_sorted=True)
            c = jax.ops.segment_sum(jnp.ones((data.shape[0], 1), data.dtype), seg, num_segments=num_segments, indices_are_sorted=True)
            return s / jnp.maximum(c, 1.0)
        key = jax.random.key(seed)
        ks = jax.random.split(key, 12)
        n_embed = jax.random.normal(ks[0], (N_NODES, D_NODE), dtype=jnp.float32)
        e_embed = jax.random.normal(ks[1], (N_EDGES, D_EDGE), dtype=jnp.float32)
        senders = jnp.sort(jax.random.randint(ks[2], (N_EDGES,), 0, N_NODES))
        receivers = jax.random.randint(ks[3], (N_EDGES,), 0, N_NODES)
        dims = _auto_mlp_dims(2 * D_NODE, OUT_DIM, N_LAYERS)
        in_dims = [2 * D_NODE] + dims[:-1]
        params = {}
        for i, (di, do) in enumerate(zip(in_dims, dims)):
            params[f'W{i}'] = jax.random.normal(ks[4 + i], (di, do), dtype=jnp.float32) / np.sqrt(di)
            params[f'b{i}'] = jnp.zeros((do,), dtype=jnp.float32)
        params['Wg'] = jax.random.normal(ks[10], (D_EDGE, dims[-1]), dtype=jnp.float32) / np.sqrt(D_EDGE)
        return dict(n_embed=n_embed, e_embed=e_embed, senders=senders, receivers=receivers, **params)
    _L1_gnn_all = _L1_gnn_setup()
    _L1_gnn_in = {k: v for k, v in _L1_gnn_all.items() if k in ('W0', 'b0', 'W1', 'b1', 'W2', 'b2', 'Wg')}
    del _L1_gnn_all
    return {'x': x, 'src': src, 'dst': dst, 'edge_attr_128': edge_attr_128, 'edge_attr_32': edge_attr_32, 'L0_gnn_lin_W': _L0_gnn_in['lin_W'], 'L0_gnn_att_src': _L0_gnn_in['att_src'], 'L0_gnn_att_dst': _L0_gnn_in['att_dst'], 'L0_gnn_lin_edge_W': _L0_gnn_in['lin_edge_W'], 'L0_gnn_att_edge': _L0_gnn_in['att_edge'], 'L0_gnn_bias': _L0_gnn_in['bias'], 'L1_gnn_W0': _L1_gnn_in['W0'], 'L1_gnn_b0': _L1_gnn_in['b0'], 'L1_gnn_W1': _L1_gnn_in['W1'], 'L1_gnn_b1': _L1_gnn_in['b1'], 'L1_gnn_W2': _L1_gnn_in['W2'], 'L1_gnn_b2': _L1_gnn_in['b2'], 'L1_gnn_Wg': _L1_gnn_in['Wg']}

def reference(x, src, dst, edge_attr_128, edge_attr_32, L0_gnn_lin_W, L0_gnn_att_src, L0_gnn_att_dst, L0_gnn_lin_edge_W, L0_gnn_att_edge, L0_gnn_bias, L1_gnn_W0, L1_gnn_b0, L1_gnn_W1, L1_gnn_b1, L1_gnn_W2, L1_gnn_b2, L1_gnn_Wg):
    import jax
    import jax.numpy as jnp

    def _L0_gnn_ref(x, edge_index, edge_attr, lin_W, att_src, att_dst, lin_edge_W, att_edge, bias):
        import jax, jax.numpy as jnp
        import numpy as np
        N = 625
        E = 10000
        IN_DIM = 256
        OUT_DIM = 64
        HEADS = 4
        EDGE_DIM = 32
        NEG_SLOPE = 0.2

        def _gat_forward(x, edge_attr, lin_W, att_src, att_dst, lin_edge_W, att_edge, bias, edge_index):
            n = x.shape[0]
            loops = jnp.arange(n, dtype=edge_index.dtype)
            ei = jnp.concatenate([edge_index, jnp.stack([loops, loops])], axis=1)
            ea = jnp.concatenate([edge_attr, jnp.zeros((n, edge_attr.shape[1]), edge_attr.dtype)], axis=0)
            src, dst = (ei[0], ei[1])
            x_proj = (x @ lin_W.T).reshape(n, HEADS, OUT_DIM)
            s_src = jnp.einsum('nhd,hd->nh', x_proj, att_src)
            s_dst = jnp.einsum('nhd,hd->nh', x_proj, att_dst)
            att = s_src[src] + s_dst[dst]
            e_proj = (ea @ lin_edge_W.T).reshape(-1, HEADS, OUT_DIM)
            att = att + jnp.einsum('ehd,hd->eh', e_proj, att_edge)
            att = jnp.where(att >= 0, att, NEG_SLOPE * att)
            seg_max = jax.ops.segment_max(att, dst, num_segments=n)
            exps = jnp.exp(att - seg_max[dst])
            denom = jax.ops.segment_sum(exps, dst, num_segments=n)
            alpha = exps / (denom[dst] + 1e-12)
            m = x_proj[src] * alpha[:, :, None]
            out = jax.ops.segment_sum(m, dst, num_segments=n)
            out = out.reshape(n, HEADS * OUT_DIM) + bias
            return out
        return _gat_forward(x, edge_attr, lin_W, att_src, att_dst, lin_edge_W, att_edge, bias, edge_index)

    def _L1_gnn_ref(n_embed, e_embed, senders, receivers, W0, b0, W1, b1, W2, b2, Wg):
        import jax, jax.numpy as jnp
        import numpy as np
        N_NODES = 512
        N_EDGES = 8192
        D_NODE = 256
        D_EDGE = 128
        OUT_DIM = 256
        N_LAYERS = 3

        def _auto_mlp_dims(inp_dim, out_dim, n_layers):
            dims = np.logspace(np.log(inp_dim), np.log(out_dim), n_layers + 1, base=np.e)
            return [int(d) for d in np.round(dims)[1:]]

        def _segment_mean(data, seg, num_segments):
            s = jax.ops.segment_sum(data, seg, num_segments=num_segments, indices_are_sorted=True)
            c = jax.ops.segment_sum(jnp.ones((data.shape[0], 1), data.dtype), seg, num_segments=num_segments, indices_are_sorted=True)
            return s / jnp.maximum(c, 1.0)
        h = jnp.concatenate([n_embed[senders], n_embed[receivers]], axis=-1)
        h = jnp.tanh(h @ W0 + b0)
        h = jnp.tanh(h @ W1 + b1)
        h = h @ W2 + b2
        h = h * (e_embed @ Wg)
        return _segment_mean(h, senders, n_embed.shape[0])
    edge_index = jnp.stack([src, dst])
    x = _layernorm(x + _L0_gnn_ref(x, edge_index, edge_attr_32, L0_gnn_lin_W, L0_gnn_att_src, L0_gnn_att_dst, L0_gnn_lin_edge_W, L0_gnn_att_edge, L0_gnn_bias), axis=-1)
    x = _layernorm(x + _L1_gnn_ref(x, edge_attr_128, src, dst, L1_gnn_W0, L1_gnn_b0, L1_gnn_W1, L1_gnn_b1, L1_gnn_W2, L1_gnn_b2, L1_gnn_Wg), axis=-1)
    return x

_drawn_inputs = setup_inputs


def setup_inputs(seed=0):
    import zlib

    import numpy as np

    out = dict(_drawn_inputs(seed))
    spreads = {'L0_gnn_bias': (0.0, 0.1),
     'L1_gnn_b0': (0.0, 0.1),
     'L1_gnn_b1': (0.0, 0.1),
     'L1_gnn_b2': (0.0, 0.1)}
    factors = {}
    for name, (base, spread) in spreads.items():
        noise = np.random.default_rng([zlib.crc32(name.encode()), seed]).standard_normal(out[name].shape)
        drawn = base * np.exp(spread * noise) if base else spread * noise
        out[name] = jnp.asarray(drawn.astype(out[name].dtype))
    for name, factor in factors.items():
        out[name] = (out[name] * factor).astype(out[name].dtype)
    return out
```

```python
from contextlib import ExitStack

import concourse.bass as bass
from concourse import mybir

P = 128
G = 4
HEADS = 4
NEG_SLOPE = 0.2
EPS = 1e-5
BIG = 3e38


class Count:

    def __init__(self, eng, sem):
        self.eng, self.sem, self.base, self.n = eng, sem, 0, 0

    def at(self, base):
        self.base, self.n = base, 0

    def did(self, ins):
        self.n += 1
        ins.then_inc(self.sem, 1)

    def wait(self):
        self.eng.wait_ge(self.sem, self.base + self.n)

    def step(self, ins):
        self.did(ins)
        self.wait()


def pieces(total, size):
    return [(a, min(size, total - a)) for a in range(0, total, size)]


def gnn_kernel(nc, x, src, dst, e128, e32, lin_W, att_src, att_dst, lin_edge_W, att_edge, bias,
               W0, b0, W1, b1, W2, b2, Wg, out):
    f32, f16, i32, f32r = mybir.dt.float32, mybir.dt.float16, mybir.dt.int32, mybir.dt.float32r
    ALU, ACT, AX = mybir.AluOpType, mybir.ActivationFunctionType, mybir.AxisListType

    N, D = x.shape
    HD = D // HEADS
    KE = e32.shape[1]
    GROUPS = N // (G * P) + 1
    NT = G * GROUPS
    NP = NT * P
    PAIRS = GROUPS // 2
    PEEL = 2
    assert GROUPS % 2 == 0 and D == 2 * P and KE * G == P and e128.shape[1] == P
    TAIL_TILES, TAIL_ROWS = divmod(N - (GROUPS - 1) * G * P, P)
    F0, F1 = W0.shape[1], W1.shape[1]
    C0, C1 = -(-F0 // 4), -(-F1 // 3)
    M0, M1 = pieces(F0, C0), pieces(F1, C1)
    assert M1[-1][1] < C1
    XW = D + 2 * HEADS
    MW = D + HEADS
    CW = D + 2 * HEADS
    HW = D + 2
    OOB = 2.0 ** 20

    XP = nc.dram_tensor("XP", (NP, D), f32, kind="Internal").ap()
    SS = nc.dram_tensor("SS", (NP, 8), f32, kind="Internal").ap()
    DS = nc.dram_tensor("DS", (NP + 2, 8), f32, kind="Internal").ap()
    ES = nc.dram_tensor("ES", (NP + 1, 4), i32, kind="Internal").ap()
    VS = nc.dram_tensor("VS", (4, HEADS, NT), f32, kind="Internal").ap()
    CS = nc.dram_tensor("CS", (2, HEADS, NT + 1), f32, kind="Internal").ap()
    DW = nc.dram_tensor("DW", (NP, 12), f32, kind="Internal").ap()
    CT = nc.dram_tensor("CT", (NP + 1, CW), f32, kind="Internal").ap()
    X1 = nc.dram_tensor("X1", (NP, D), f32, kind="Internal").ap()

    def tiles(a, g, n=G):
        return a[bass.ds(g * (G * P), n * P), :].rearrange("(t p) w -> p t w", p=P)

    def shifted(a, g, by):
        return a[bass.ds(g * (G * P) + by, G * P), :].rearrange("(t p) w -> p t w", p=P)

    def groups(eng, body):
        for g in range(2 * PEEL):
            body(g, g % 2, g // 2, False)
        with eng.Fori(PEEL, PAIRS - 1) as i:
            for s in range(2):
                body(i * 2 + s, s, i, False)
        for s in range(2):
            body(2 * PAIRS - 2 + s, s, PAIRS - 1, s == 1)

    def need(eng, sem, n):
        if not (isinstance(n, int) and n <= 0):
            eng.wait_ge(sem, n)

    def early(g, n):
        return isinstance(g, int) and g < n

    def late(g, n):
        return isinstance(g, int) and g + n >= GROUPS

    def load_rows(eng, buf, a, g, last, sem):
        if not last:
            eng.dma_start(buf[:, :, :], tiles(a, g)).then_inc(sem, 16)
            return
        eng.dma_start(buf[:, 0:TAIL_TILES, :], tiles(a, g, TAIL_TILES)).then_inc(sem, 16)
        r0 = N - TAIL_ROWS
        eng.dma_start(buf[0:TAIL_ROWS, TAIL_TILES, :], a[r0:N, :]).then_inc(sem, 16)

    top = ExitStack()
    with top:
        def alloc(stack, name, shape, dt=f32):
            return stack.enter_context(nc.sbuf_tensor(name, shape, dt))

        def sem(name):
            return top.enter_context(nc.semaphore(name))

        def sems(name, n=2):
            return [sem(f"{name}{i}") for i in range(n)]

        turn = sem("pool_turn")
        dturn = sem("dve_turn")

        B = [top.enter_context(nc.psum_tensor(f"bank{i}", [P, 512], f32)) for i in range(8)]

        ident = alloc(top, "ident", [P, P])
        identh = alloc(top, "identh", [P, P], f16)
        ones = alloc(top, "ones", [P, P])
        before = alloc(top, "before", [P, P])
        after = alloc(top, "after", [P, P])
        iota = alloc(top, "iota", [P, max(NT, P)], f16)
        is127 = alloc(top, "is127", [P, 2])
        wst = alloc(top, "wst", [P, 2, XW])
        wedge = alloc(top, "wedge", [P, 4 * HEADS])
        biasb = alloc(top, "biasb", [P, D])
        w0r = [alloc(top, f"w0r{k}", [P, 4, F0], f32r) for k in range(2)]
        w1r = [alloc(top, f"w1r{k}", [C0, 4, F1], f32r) for k in range(2)]
        w2r = [alloc(top, f"w2r{k}", [C1, 3, D], f32r) for k in range(2)]
        wgr = [alloc(top, f"wgr{k}", [P, D], f32r) for k in range(2)]
        b0s = alloc(top, "b0s", [C0, 4])
        b1s = alloc(top, "b1s", [C1, 3])
        lastd = alloc(top, "lastd", [P, NT], i32)

        ph = ExitStack()
        with ph:
            lw = alloc(ph, "lw", [P, 2, D])
            w0s = alloc(ph, "w0s", [P, 4, F0])
            w1s = alloc(ph, "w1s", [C0, 4, F1])
            w2s = alloc(ph, "w2s", [C1, 3, D])
            wgs = alloc(ph, "wgs", [P, D])
            le4 = alloc(ph, "le4", [P, 2, 4, KE])
            ab = alloc(ph, "ab", [P, 2, 3 * HEADS])
            ioi = alloc(ph, "ioi", [P, max(NT, P)], i32)
            s_zero, s_load, s_const = sem("w_zero"), sem("w_load"), sem("w_const")
            s_attl, s_mm, s_ev = sem("w_att"), sem("w_mm"), sem("w_ev")
            with nc.Block() as block:
                @block.gpsimd
                def _(pool):
                    c = Count(pool, s_const)
                    c.did(nc.gpsimd.memset(ident[:], 0.0))
                    c.did(nc.gpsimd.memset(ones[:], 1.0))
                    c.did(nc.gpsimd.memset(before[:], 1.0))
                    c.did(nc.gpsimd.memset(after[:], 1.0))
                    c.did(nc.gpsimd.memset(is127[:, 0:1], 0.0))
                    c.did(nc.gpsimd.memset(is127[:, 1:2], -1.0))
                    c.did(nc.gpsimd.iota(ioi[:], pattern=[[1, max(NT, P)]], base=0, channel_multiplier=0))
                    c.wait()
                    c.did(nc.gpsimd.affine_select(out=ident[:], in_=ident[:], compare_op=ALU.not_equal,
                                                  fill=1.0, base=0, pattern=[[-1, P]], channel_multiplier=1))
                    c.did(nc.gpsimd.affine_select(out=before[:], in_=before[:], compare_op=ALU.is_gt,
                                                  fill=0.0, base=0, pattern=[[-1, P]], channel_multiplier=1))
                    c.did(nc.gpsimd.affine_select(out=after[:], in_=after[:], compare_op=ALU.is_gt,
                                                  fill=0.0, base=0, pattern=[[1, P]], channel_multiplier=-1))
                    for k in range(2):
                        c.did(nc.gpsimd.affine_select(out=is127[:, k:k + 1], in_=is127[:, k:k + 1],
                                                      compare_op=ALU.not_equal, fill=1.0 - k, base=1 - P,
                                                      pattern=[[0, 1]], channel_multiplier=1))
                    c.did(nc.gpsimd.tensor_copy(iota[:], ioi[:]))
                    c.wait()
                    c.did(nc.gpsimd.tensor_copy(identh[:], ident[:]))

                @block.sync
                def _(sp):
                    sp.wait_ge(s_zero, 1)
                    with nc.allow_non_contiguous_dma(reason="small weight vectors"):
                        for k, a in enumerate((att_src, att_dst, att_edge)):
                            for h in range(HEADS):
                                r = (h % 2) * HD
                                sp.dma_start(ab[r:r + HD, h // 2, k * HEADS + h:k * HEADS + h + 1],
                                             a[h, :].rearrange("(d a) -> d a", a=1)).then_inc(s_attl, 16)
                        for k, (a, n) in enumerate(M0):
                            sp.dma_start(b0s[0:n, k:k + 1], b0[a:a + n].rearrange("(d a) -> d a", a=1))\
                                .then_inc(s_load, 16)
                        for k, (a, n) in enumerate(M1):
                            sp.dma_start(b1s[0:n, k:k + 1], b1[a:a + n].rearrange("(d a) -> d a", a=1))\
                                .then_inc(s_load, 16)
                    sp.wait_ge(s_load, 16 * 7)

                @block.scalar
                def _(act):
                    act.dma_start(lw[:], lin_W.rearrange("(c p) i -> p c i", p=P)).then_inc(s_attl, 16)
                    for r in range(4):
                        act.dma_start(le4[:, :, r, :], lin_edge_W.rearrange("(c p) k -> p c k", p=P))\
                            .then_inc(s_attl, 16)
                    act.dma_start(biasb[:], bias.partition_broadcast(P)).then_inc(s_attl, 16)
                    act.dma_start(w0s[:], W0.rearrange("(c p) m -> p c m", p=P)).then_inc(s_attl, 16)
                    for k, (a, n) in enumerate(M0):
                        act.dma_start(w1s[0:n, k, :], W1[a:a + n, :]).then_inc(s_attl, 16)
                    for k, (a, n) in enumerate(M1):
                        act.dma_start(w2s[0:n, k, :], W2[a:a + n, :]).then_inc(s_attl, 16)
                    a, n = M1[-1]
                    act.dma_start(w2s[n:n + 1, 2, :], b2.rearrange("(a d) -> a d", a=1)).then_inc(s_attl, 16)
                    act.dma_start(wgs[:], Wg).then_inc(s_attl, 16)
                    act.wait_ge(s_attl, 16 * (3 * HEADS + 16))

                @block.vector
                def _(dve):
                    nc.vector.memset(ab[:], 0.0).then_inc(s_zero, 1)
                    c = Count(dve, s_ev)
                    c.did(nc.vector.memset(wedge[:], 0.0))
                    dve.wait_ge(s_attl, 16 * (3 * HEADS + 16))
                    parts = [(w0r, w0s, P, slice(0, 4)), (wgr, wgs, P, None)]
                    parts += [(w1r, w1s, n, k) for k, (a, n) in enumerate(M0)]
                    parts += [(w2r, w2s, n + (k == 2), k) for k, (a, n) in enumerate(M1)]
                    for low in range(2):
                        for w, full, n, k in parts:
                            hi, lo, f = (t[0:n] if k is None else t[0:n, k, :] for t in (w[0], w[1], full))
                            if low:
                                c.did(nc.vector.tensor_tensor(lo, f, hi.bitcast(f32), ALU.subtract))
                            else:
                                c.did(nc.vector.tensor_copy(hi, f))
                        c.wait()
                    dve.wait_ge(s_mm, 1)
                    for k in range(2):
                        c.did(nc.vector.tensor_copy(wst[:, k, 0:D], B[k][:, 0:D]))
                    dve.wait_ge(s_mm, 2)
                    for k in range(2):
                        c.did(nc.vector.tensor_copy(wst[:, k, D:XW], B[2 + k][:, 0:8]))
                    c.wait()
                    for r in range(4):
                        c.did(nc.vector.tensor_copy(wedge[r * KE:(r + 1) * KE, r * HEADS:(r + 1) * HEADS],
                                                    B[4][r * KE:(r + 1) * KE, 0:HEADS]))

                @block.tensor
                def _(pe):
                    pe.wait_ge(s_const, 12)
                    pe.wait_ge(s_attl, 16 * (3 * HEADS + 16))
                    for k in range(2):
                        for c in range(2):
                            t = nc.tensor.transpose(B[k][:, c * P:(c + 1) * P], lw[:, c, k * P:(k + 1) * P], ident[:])
                    t.then_inc(s_mm, 1)
                    for k in range(2):
                        for c in range(2):
                            nc.tensor.matmul(B[2 + k][:, 0:8], lw[:, c, k * P:(k + 1) * P], ab[:, c, 0:8],
                                             start=(c == 0), stop=(c == 1))
                    for c in range(2):
                        t = nc.tensor.matmul(B[4][:, 0:HEADS], le4[:, c, :, :].rearrange("p r k -> p (r k)"),
                                             ab[:, c, 8:12], start=(c == 0), stop=(c == 1))
                    t.then_inc(s_mm, 1)

        ph = ExitStack()
        with ph:
            xin = [alloc(ph, f"xin{s}", [P, G, D]) for s in range(2)]
            xT = [alloc(ph, f"xT{s}", [P, 2, G * P]) for s in range(2)]
            xps = [alloc(ph, f"xps{s}", [P, G, XW]) for s in range(2)]
            x_loaded, xp_stored = sems("p_x_loaded"), sems("p_xp_stored")
            xt_psum, xt_d, xt_a = sem("p_xt_psum"), sem("p_xt_dve"), sem("p_xt_act")
            pr_psum, pr_d, pr_a = sem("p_pr_psum"), sem("p_pr_dve"), sem("p_pr_act")
            with nc.Block() as block:
                @block.sync
                def _(sp):
                    def body(g, s, i, last):
                        need(sp, xt_psum, 2 * (g - 1))
                        load_rows(sp, xin[s], x, g, last, x_loaded[s])
                    groups(sp, body)

                @block.tensor
                def _(pe):
                    def body(g, s, i, last):
                        pe.wait_ge(x_loaded[s], 16 * (i + 1) + 16 * last)
                        need(pe, xt_d, g - 1)
                        need(pe, xt_a, g - 1)
                        for k in range(2):
                            for j in range(G):
                                t = nc.tensor.transpose(B[2 * s + k][:, j * P:(j + 1) * P],
                                                        xin[s][:, j, k * P:(k + 1) * P], ident[:])
                            t.then_inc(xt_psum, 1)
                        pe.wait_ge(xt_d, g + 1)
                        pe.wait_ge(xt_a, g + 1)
                        for j in range(G):
                            need(pe, (pr_d, pr_a)[j % 2], 2 * g + j // 2 - 1)
                            for k in range(2):
                                t = nc.tensor.matmul(B[4 + j][:, 0:XW], xT[s][:, k, j * P:(j + 1) * P], wst[:, k, :],
                                                     start=(k == 0), stop=(k == 1))
                            t.then_inc(pr_psum, 1)
                    groups(pe, body)

                @block.vector
                def _(dve):
                    def body(g, s, i, last):
                        need(dve, pr_psum, 4 * (g - 1))
                        dve.wait_ge(xt_psum, 2 * g + 1)
                        nc.vector.tensor_copy(xT[s][:, 0, :], B[2 * s][:]).then_inc(xt_d, 1)
                        need(dve, xp_stored[s], 32 * i)
                        for j in (0, 2):
                            dve.wait_ge(pr_psum, 4 * g + j + 1)
                            nc.vector.tensor_copy(xps[s][:, j, :], B[4 + j][:, 0:XW]).then_inc(pr_d, 1)
                    groups(dve, body)

                @block.scalar
                def _(act):
                    def body(g, s, i, last):
                        need(act, pr_psum, 4 * (g - 1))
                        act.wait_ge(xt_psum, 2 * g + 2)
                        nc.scalar.copy(xT[s][:, 1, :], B[2 * s + 1][:]).then_inc(xt_a, 1)
                        need(act, xp_stored[s], 32 * i)
                        for j in (1, 3):
                            act.wait_ge(pr_psum, 4 * g + j + 1)
                            nc.scalar.copy(xps[s][:, j, :], B[4 + j][:, 0:XW]).then_inc(pr_a, 1)
                    groups(act, body)

                @block.gpsimd
                def _(pool):
                    def body(g, s, i, last):
                        pool.wait_ge(pr_d, 2 * g + 2)
                        pool.wait_ge(pr_a, 2 * g + 2)
                        pool.sem_inc(turn, 1)
                        pool.dma_start(tiles(XP, g), xps[s][:, :, 0:D]).then_inc(xp_stored[s], 16)
                        pool.dma_start(tiles(SS, g), xps[s][:, :, D:XW]).then_inc(xp_stored[s], 16)
                    groups(pool, body)
                    for s in range(2):
                        pool.wait_ge(xp_stored[s], 32 * PAIRS)
        NC = -(-NT // P)
        srt = ExitStack()
        with srt:
            keys = (dst, src)
            KI = [alloc(srt, f"key_int{q}", [P, NT], i32) for q in range(2)]
            KF = [alloc(srt, f"key{q}", [P, NT]) for q in range(2)]
            LO = [alloc(srt, f"key_lo{q}", [P, NT]) for q in range(2)]
            HI = [alloc(srt, f"key_hi{q}", [P, NT]) for q in range(2)]
            start = [alloc(srt, f"start{q}", [P, NT]) for q in range(2)]
            eid = alloc(srt, "eid", [P, NT], i32)
            ohlo = [[alloc(srt, f"ohlo{q}{s}", [P, G, P], f16) for s in range(2)] for q in range(2)]
            ohhi = [[alloc(srt, f"ohhi{q}{s}", [P, G, NT], f16) for s in range(2)] for q in range(2)]

            def one_hots(dve, g, s, done):
                for q in range(2):
                    for j in range(G):
                        t = bass.ds(g * G + j, 1)
                        nc.vector.tensor_scalar(ohlo[q][s][:, j, :], iota[:, 0:P], LO[q][:, t], None, ALU.is_equal)
                        o = nc.vector.tensor_scalar(ohhi[q][s][:, j, :], iota[:, 0:NT], HI[q][:, t], None, ALU.is_equal)
                o.then_inc(done, 1)

            ph = ExitStack()
            with ph:
                kr = [alloc(ph, f"key_rows{q}", [P, NC, P], i32) for q in range(2)]
                krf = [alloc(ph, f"key_rowsf{q}", [P, NC, P]) for q in range(2)]
                ki = [alloc(ph, f"key_digit{q}", [P, NT], i32) for q in range(4)]
                hist = [alloc(ph, f"hist{q}", [P, NT]) for q in range(2)]
                tot = [alloc(ph, f"tot{q}", [P, NT]) for q in range(2)]
                cum = [alloc(ph, f"cum{q}", [P, NT]) for q in range(2)]
                eid0 = alloc(ph, "eid0", [P, NT], i32)
                sent = alloc(ph, "sentinel", [1, 8])
                senti = alloc(ph, "sentinel_int", [1, 4], i32)
                h_pad, h_loaded, h_rows, h_psum = sem("h_pad"), sem("h_loaded"), sem("h_rows"), sem("h_psum")
                h_chain, h_oh, h_acc, h_hist, h_sums = sem("h_chain"), sem("h_oh"), sem("h_acc"), sem("h_hist"), sem("h_sums")
                fr, rr = divmod(N, P)
                loads = [(c, min(P, fr - c * P)) for c in range(NC) if fr - c * P > 0]
                with nc.Block() as block:
                    @block.gpsimd
                    def _(pool):
                        for q in range(2):
                            nc.gpsimd.memset(kr[q][:], N).then_inc(h_pad, 1)
                        nc.gpsimd.memset(sent[:], -1.0).then_inc(h_pad, 1)
                        nc.gpsimd.memset(senti[:], -1).then_inc(h_pad, 1)
                        nc.gpsimd.iota(eid0[:], pattern=[[P, NT]], base=0, channel_multiplier=1).then_inc(h_pad, 1)

                    @block.sync
                    def _(sp):
                        sp.wait_ge(h_pad, 4)
                        for q in range(2):
                            for c, n in loads:
                                sp.dma_start(kr[q][0:n, c, :], keys[q][c * P * P:(c * P + n) * P]
                                             .rearrange("(t p) -> t p", p=P)).then_inc(h_loaded, 16)
                            sp.dma_start(kr[q][fr % P:fr % P + 1, fr // P, 0:rr],
                                         keys[q][fr * P:N].rearrange("(a p) -> a p", a=1)).then_inc(h_loaded, 16)
                        sp.dma_start(DS[0:1, :], sent[:]).then_inc(h_loaded, 16)
                        sp.dma_start(DS[NP + 1:NP + 2, :], sent[:]).then_inc(h_loaded, 16)
                        sp.dma_start(ES[NP:NP + 1, :], senti[:]).then_inc(h_loaded, 16)
                        sp.wait_ge(h_loaded, 16 * (2 * len(loads) + 5))

                    @block.vector
                    def _(dve):
                        c = Count(dve, h_chain)
                        dve.wait_ge(h_loaded, 16 * (2 * len(loads) + 5))
                        for q in range(2):
                            nc.vector.tensor_copy(krf[q][:], kr[q][:]).then_inc(h_rows, 1)
                        dve.wait_ge(h_pad, 5)
                        c.did(nc.vector.tensor_scalar(eid[:], eid0[:], N - 1, None, ALU.min))
                        dve.wait_ge(h_psum, 1)
                        for q in range(2):
                            c.did(nc.vector.tensor_copy(KF[q][:], B[q][:, 0:NT]))
                            c.did(nc.vector.tensor_copy(KI[q][:], B[q][:, 0:NT]))
                        c.wait()
                        for q in range(2):
                            c.did(nc.vector.tensor_scalar(ki[q][:], KI[q][:], P - 1, None, ALU.bitwise_and))
                            c.did(nc.vector.tensor_scalar(ki[2 + q][:], KI[q][:], 7, None, ALU.arith_shift_right))
                        c.wait()
                        for q in range(2):
                            c.did(nc.vector.tensor_copy(LO[q][:], ki[q][:]))
                            c.did(nc.vector.tensor_copy(HI[q][:], ki[2 + q][:]))
                        c.wait()

                        def body(g, s, i, last):
                            need(dve, h_acc, g - 1)
                            one_hots(dve, g, s, h_oh)
                        groups(dve, body)
                        dve.wait_ge(h_acc, GROUPS)
                        for q in range(2):
                            nc.vector.tensor_copy(hist[q][:], B[q][:, 0:NT]).then_inc(h_hist, 1)
                        dve.wait_ge(h_sums, 1)
                        for q in range(2):
                            c.did(nc.vector.tensor_copy(tot[q][:], B[2 + q][:, 0:NT]))
                        c.wait()
                        for q in range(2):
                            c.did(nc.vector.tensor_tensor_scan(cum[q][:], tot[q][:], tot[q][:], 0.0, ALU.add, ALU.max))
                        c.wait()
                        for q in range(2):
                            c.did(nc.vector.tensor_tensor(cum[q][:], cum[q][:], tot[q][:], ALU.subtract))
                        c.wait()
                        for q in range(2):
                            c.did(nc.vector.tensor_tensor(start[q][:], cum[q][:], B[4 + q][:, 0:NT], ALU.add))
                        c.wait()
                        c.step(nc.vector.scalar_tensor_tensor(tot[0][:], start[0][:], -1.0 - NP, hist[0][:],
                                                              ALU.add, ALU.add))
                        c.step(nc.vector.scalar_tensor_tensor(tot[1][:], hist[0][:], 0.0, tot[0][:],
                                                              ALU.is_gt, ALU.mult))
                        c.did(nc.vector.tensor_scalar(lastd[:], tot[1][:], float(NP), None, ALU.add))

                    @block.tensor
                    def _(pe):
                        pe.wait_ge(h_rows, 2)
                        for q in range(2):
                            for c in range(NC):
                                t = nc.tensor.transpose(B[q][:, c * P:(c + 1) * P], krf[q][:, c, :], ident[:])
                        t.then_inc(h_psum, 1)

                        def body(g, s, i, last):
                            pe.wait_ge(h_oh, g + 1)
                            for q in range(2):
                                for j in range(G):
                                    first = isinstance(g, int) and g == 0 and j == 0
                                    t = nc.tensor.matmul(B[q][:, 0:NT], ohlo[q][s][:, j, :], ohhi[q][s][:, j, :],
                                                         start=first, stop=last and j == G - 1)
                            t.then_inc(h_acc, 1)
                        groups(pe, body)
                        pe.wait_ge(h_hist, 2)
                        for q in range(2):
                            nc.tensor.matmul(B[2 + q][:, 0:NT], ones[:], hist[q][:], start=True, stop=True)
                            t = nc.tensor.matmul(B[4 + q][:, 0:NT], after[:], hist[q][:], start=True, stop=True)
                        t.then_inc(h_sums, 1)

            ph = ExitStack()
            with ph:
                tab = [[alloc(ph, f"table{q}{k}", [P, NT]) for k in range(2)] for q in range(2)]
                oT = [alloc(ph, f"ohloT{k}", [P, 2, P]) for k in range(2)]
                oh_psum = B[3][:, 0:P].bitcast(f16)
                kb = (2, 7)
                eqj = [alloc(ph, f"eq{q}", [P, P]) for q in range(2)]
                lkj = [alloc(ph, f"found{q}", [P, NT]) for q in range(2)]
                cnt = [[alloc(ph, f"earlier{q}{s}", [P, G]) for s in range(2)] for q in range(2)]
                rk = [[alloc(ph, f"rank{q}{s}", [P, G]) for s in range(2)] for q in range(2)]
                ri = [[alloc(ph, f"rank_int{q}{s}", [P, G], i32) for s in range(2)] for q in range(2)]
                kcol = [[alloc(ph, f"key_col{q}{s}", [P, G]) for s in range(2)] for q in range(2)]
                ix = [alloc(ph, f"ends{s}", [P, 2, G], i32) for s in range(2)]
                sg = [alloc(ph, f"sgather{s}", [P, G, 16]) for s in range(2)]
                pd = [alloc(ph, f"by_dst{s}", [P, G, 8]) for s in range(2)]
                pp = [alloc(ph, f"by_src{s}", [P, G, 4], i32) for s in range(2)]
                lg = [alloc(ph, f"logit{s}", [P, G, HEADS]) for s in range(2)]
                ein = [alloc(ph, f"ein{s}", [P, G, KE]) for s in range(2)]
                eT = [alloc(ph, f"eT{s}", [P, P]) for s in range(2)]
                e_ld, sg_ld = sems("r_e_loaded"), sems("r_s_gathered")
                ds_st, es_st = sems("r_ds_stored"), sems("r_es_stored")
                r_init, r_oh, r_ix, r_tk, r_upd = sem("r_init"), sem("r_oh"), sem("r_ix"), sem("r_tk"), sem("r_upd")
                r_ott = sem("r_ott")
                r_look, r_ot, r_tab, r_eq, r_rank = sem("r_look"), sem("r_ot"), sem("r_tab"), sem("r_eq"), sem("r_rank")
                r_et, r_eta, r_ae, r_pay, r_ch = sem("r_et"), sem("r_et_act"), sem("r_ae"), sem("r_pay"), sem("r_chain")
                with nc.Block() as block:
                    @block.sync
                    def _(sp):
                        def body(g, s, i, last):
                            need(sp, r_et, g - 1)
                            load_rows(sp, ein[s], e32, g, last, e_ld[s])
                        groups(sp, body)

                    @block.gpsimd
                    def _(pool):
                        def scatters(g, s):
                            pool.wait_ge(r_pay, g + 1)
                            pool.sem_inc(turn, 1)
                            for j in range(G):
                                pool.indirect_dma_start(
                                    out=DS, out_offset=bass.IndirectOffsetOnAxis(ap=ri[0][s][:, j:j + 1], axis=0),
                                    in_=pd[s][:, j, :], in_offset=None).then_inc(ds_st[s], 16)
                                pool.indirect_dma_start(
                                    out=ES, out_offset=bass.IndirectOffsetOnAxis(ap=ri[1][s][:, j:j + 1], axis=0),
                                    in_=pp[s][:, j, :], in_offset=None).then_inc(es_st[s], 16)

                        def body(g, s, i, last):
                            pool.wait_ge(r_ix, g + 1)
                            pool.sem_inc(turn, 1)
                            for j in range(G):
                                for k in range(2):
                                    pool.indirect_dma_start(
                                        out=sg[s][:, j, 8 * k:8 * k + 8], out_offset=None, in_=SS,
                                        in_offset=bass.IndirectOffsetOnAxis(ap=ix[s][:, k, j:j + 1], axis=0))\
                                        .then_inc(sg_ld[s], 16)
                            if not early(g, 1):
                                scatters(g - 1, 1 - s)
                        groups(pool, body)
                        scatters(GROUPS - 1, 1)
                        for s in range(2):
                            pool.wait_ge(ds_st[s], 16 * G * PAIRS)
                            pool.wait_ge(es_st[s], 16 * G * PAIRS)

                    @block.scalar
                    def _(act):
                        def body(g, s, i, last):
                            for j in range(G):
                                t, b = g * G + j, j % 2
                                for q in range(2):
                                    if isinstance(t, int) and t == 0:
                                        act.wait_ge(r_init, 1)
                                    need(act, r_upd, 2 * t + q - 1)
                                    need(act, r_look, 2 * (t - 1) + q - 1)
                                    nc.scalar.copy(tab[q][b][:], B[q][:, 0:NT]).then_inc(r_tab, 1)
                                act.wait_ge(r_ott, t + 1)
                                nc.scalar.copy(oT[b][:].rearrange("p q n -> p (q n)"), oh_psum).then_inc(r_ot, 1)
                            act.wait_ge(r_et, g + 1)
                            nc.scalar.copy(eT[s][:], B[6][:, 0:P]).then_inc(r_eta, 1)
                        groups(act, body)

                    @block.tensor
                    def _(pe):
                        for q in range(2):
                            t = nc.tensor.matmul(B[q][:, 0:NT], ident[:], start[q][:], start=True, stop=True)
                        t.then_inc(r_init, 1)

                        def body(g, s, i, last):
                            pe.wait_ge(r_oh, g + 1)
                            for j in range(G):
                                t, b = g * G + j, j % 2
                                need(pe, r_ot, t)
                                for q in range(2):
                                    o = nc.tensor.transpose(oh_psum[:, q * P:(q + 1) * P], ohlo[q][s][:, j, :],
                                                            identh[:])
                                o.then_inc(r_ott, 1)
                                need(pe, r_eq, 2 * (t - 1))
                                for q in range(2):
                                    o = nc.tensor.transpose(B[kb[b]][:, q * P:(q + 1) * P],
                                                            kcol[q][s][:, j:j + 1].to_broadcast([P, P]), ident[:])
                                o.then_inc(r_tk, 1)
                                for q in range(2):
                                    pe.wait_ge(r_tab, 2 * t + q + 1)
                                    nc.tensor.matmul(B[q][:, 0:NT], ohlo[q][s][:, j, :], ohhi[q][s][:, j, :],
                                                     start=False, stop=True,
                                                     skip_group_check=True).then_inc(r_upd, 1)
                                for q in range(2):
                                    pe.wait_ge(r_ot, t + 1)
                                    need(pe, r_rank, 2 * (t - 1) + q + 1)
                                    nc.tensor.matmul(B[4 + q][:, 0:NT], oT[b][:, q, :], tab[q][b][:],
                                                     start=True, stop=True).then_inc(r_look, 1)
                            pe.wait_ge(e_ld[s], 16 * (i + 1) + 16 * last)
                            need(pe, r_pay, g)
                            nc.tensor.transpose(B[6][:, 0:P], ein[s][:, :, :].rearrange("p t k -> p (t k)"), ident[:])\
                                .then_inc(r_et, 1)
                            pe.wait_ge(r_eta, g + 1)
                            nc.tensor.matmul(B[6][:, 256:256 + G * HEADS], eT[s][:], wedge[:],
                                             start=True, stop=True).then_inc(r_ae, 1)
                        groups(pe, body)

                    @block.vector
                    def _(dve):
                        c = Count(dve, r_ch)
                        for s in range(2):
                            c.did(nc.vector.memset(pd[s][:], 0.0))
                            c.did(nc.vector.memset(pp[s][:], 0))
                        c.wait()
                        base0, STEPS = c.n, 12

                        def body(g, s, i, last):
                            c.at(base0 + g * STEPS)
                            t4 = bass.ds(g * G, G)
                            need(dve, r_look, 8 * (g - 1))
                            for q in range(2):
                                c.did(nc.vector.tensor_copy(kcol[q][s][:], KF[q][:, t4]))
                            c.did(nc.vector.tensor_copy(ix[s][:, 0, :], KI[1][:, t4]))
                            c.wait()
                            nc.vector.tensor_copy(ix[s][:, 1, :], KI[0][:, t4]).then_inc(r_ix, 1)
                            one_hots(dve, g, s, r_oh)
                            for j in range(G):
                                t = g * G + j
                                for q in range(2):
                                    dve.wait_ge(r_tk, t + 1)
                                    nc.vector.scalar_tensor_tensor(eqj[q][:], B[kb[j % 2]][:, q * P:(q + 1) * P], kcol[q][s][:, j:j + 1],
                                                                   before[:], ALU.is_equal, ALU.mult,
                                                                   accum_out=cnt[q][s][:, j:j + 1]).then_inc(r_eq, 1)
                                for q in range(2):
                                    dve.wait_ge(r_look, 2 * t + q + 1)
                                    dve.wait_ge(r_eq, 2 * t + q + 1)
                                    nc.vector.tensor_tensor_reduce(
                                        out=lkj[q][:], in0=B[4 + q][:, 0:NT], in1=ohhi[q][s][:, j, :], scale=1.0,
                                        scalar=cnt[q][s][:, j:j + 1], op0=ALU.mult, op1=ALU.add,
                                        accum_out=rk[q][s][:, j:j + 1]).then_inc(r_rank, 1)
                            need(dve, ds_st[s], 16 * G * i)
                            need(dve, es_st[s], 16 * G * i)
                            dve.wait_ge(r_rank, 8 * (g + 1))
                            c.did(nc.vector.tensor_scalar(ri[0][s][:], rk[0][s][:], 1.0, None, ALU.add))
                            c.did(nc.vector.tensor_copy(ri[1][s][:], rk[1][s][:]))
                            c.did(nc.vector.tensor_copy(pp[s][:, :, 0], KI[1][:, t4]))
                            c.did(nc.vector.tensor_copy(pp[s][:, :, 1], KI[0][:, t4]))
                            c.did(nc.vector.tensor_copy(pp[s][:, :, 2], eid[:, t4]))
                            c.did(nc.vector.tensor_copy(pd[s][:, :, 0], KF[0][:, t4]))
                            c.did(nc.vector.tensor_copy(pd[s][:, :, 1].bitcast(i32), KI[1][:, t4]))
                            dve.wait_ge(sg_ld[s], 32 * G * (i + 1))
                            c.step(nc.vector.tensor_tensor(lg[s][:], sg[s][:, :, 0:HEADS], sg[s][:, :, 12:16], ALU.add))
                            dve.wait_ge(r_ae, g + 1)
                            c.step(nc.vector.tensor_tensor(
                                lg[s][:], lg[s][:], B[6][:, 256:256 + G * HEADS].rearrange("p (t h) -> p t h", t=G), ALU.add))
                            assert c.n == STEPS, c.n
                            nc.vector.scalar_tensor_tensor(pd[s][:, :, 2:6], lg[s][:], NEG_SLOPE, lg[s][:],
                                                           ALU.mult, ALU.max).then_inc(r_pay, 1)
                        groups(dve, body)
        CH = pieces(NT, P)
        ph = ExitStack()
        with ph:
            own = alloc(ph, "own", [P, NC, P, 8])
            prv = alloc(ph, "prv", [P, NC, P, 8])
            nxt = alloc(ph, "nxt", [P, NC, P, 8])
            rf = alloc(ph, "reset_f", [P, NC, P])
            rb = alloc(ph, "reset_b", [P, NC, P])
            mf = alloc(ph, "max_f", [P, NC, HEADS, P])
            mb = alloc(ph, "max_b", [P, NC, HEADS, P])
            sm = alloc(ph, "row_sums", [P, NC, 4, HEADS])
            cr = alloc(ph, "carry", [P, NC, 2, HEADS])
            rows = alloc(ph, "rows", [HEADS, 4, NT])
            cs = alloc(ph, "carries", [HEADS, 2, NT + 1])
            dwt = alloc(ph, "dwt", [P, NC, P, 12])
            dummy = alloc(ph, "no_edges", [1, CW])
            g_ld, g_sum, g_rows, g_scan = sem("g_loaded"), sem("g_summary"), sem("g_rows"), sem("g_scan")
            g_cst, g_car, g_sub, g_exp, g_st = sem("g_cs_stored"), sem("g_carry"), sem("g_sub"), sem("g_exp"), sem("g_stored")
            g_vst, g_ch = sem("g_vs_stored"), sem("g_chain")
            with nc.Block() as block:
                @block.sync
                def _(sp):
                    for c, (a, n) in enumerate(CH):
                        for k, buf in ((1, own), (0, prv), (2, nxt)):
                            sp.dma_start(buf[0:n, c, :, :].rearrange("p t w -> p (t w)"),
                                         DS[a * P + k:(a + n) * P + k, :].rearrange("(p t) w -> p (t w)", t=P))\
                                .then_inc(g_ld, 16)
                    sp.wait_ge(g_sum, 1)
                    with nc.allow_non_contiguous_dma(reason="row summaries, once"):
                        for c, (a, n) in enumerate(CH):
                            for k in range(4):
                                sp.dma_start(VS[k, :, a:a + n].rearrange("h t -> t h"), sm[0:n, c, k, :]).then_inc(g_vst, 16)
                        sp.wait_ge(g_vst, 64 * len(CH))
                        sp.dma_start(rows[:], VS.rearrange("k h t -> h k t")).then_inc(g_rows, 16)
                        sp.wait_ge(g_scan, 2)
                        sp.dma_start(CS.rearrange("k h t -> h k t"), cs[:]).then_inc(g_cst, 16)
                        sp.wait_ge(g_cst, 16)
                        for c, (a, n) in enumerate(CH):
                            for k in range(2):
                                sp.dma_start(cr[0:n, c, k, :], CS[k, :, a + k:a + k + n].rearrange("h t -> t h"))\
                                    .then_inc(g_car, 16)
                    for c, (a, n) in enumerate(CH):
                        sp.wait_ge(g_exp, c + 1)
                        sp.dma_start(DW[a * P:(a + n) * P, :].rearrange("(p t) w -> p (t w)", t=P),
                                     dwt[0:n, c, :, :].rearrange("p t w -> p (t w)")).then_inc(g_st, 16)
                    sp.dma_start(CT[NP:NP + 1, :], dummy[:]).then_inc(g_st, 16)
                    sp.wait_ge(g_st, 16 * (len(CH) + 1))

                @block.scalar
                def _(act):
                    for c, (a, n) in enumerate(CH):
                        act.wait_ge(g_sub, c + 1)
                        nc.scalar.activation(dwt[0:n, c, :, 2:6], dwt[0:n, c, :, 2:6], ACT.Exp).then_inc(g_exp, 1)

                @block.vector
                def _(dve):
                    k = Count(dve, g_ch)
                    k.did(nc.vector.memset(dwt[:], 0.0))
                    k.did(nc.vector.memset(cs[:], -BIG))
                    k.did(nc.vector.memset(dummy[:, 0:MW], 0.0))
                    k.did(nc.vector.memset(dummy[:, MW:CW], -1e30))
                    dve.wait_ge(g_ld, 48 * len(CH))
                    for c, (a, n) in enumerate(CH):
                        k.did(nc.vector.tensor_tensor(rf[0:n, c, :], own[0:n, c, :, 0], prv[0:n, c, :, 0], ALU.not_equal))
                        k.did(nc.vector.tensor_tensor(rb[0:n, c, :], own[0:n, c, :, 0], nxt[0:n, c, :, 0], ALU.not_equal))
                    k.wait()
                    for c, (a, n) in enumerate(CH):
                        k.did(nc.vector.tensor_scalar(rf[0:n, c, :], rf[0:n, c, :], -BIG, None, ALU.mult))
                        k.did(nc.vector.tensor_scalar(rb[0:n, c, :], rb[0:n, c, :], -BIG, None, ALU.mult))
                    k.wait()

                    def scans(first):
                        for c, (a, n) in enumerate(CH):
                            for h in range(HEADS):
                                k.did(nc.vector.tensor_tensor_scan(
                                    mf[0:n, c, h, :], rf[0:n, c, :], own[0:n, c, :, 2 + h],
                                    -BIG if first else cr[0:n, c, 0, h:h + 1], ALU.add, ALU.max))
                                k.did(nc.vector.tensor_tensor_scan(
                                    mb[0:n, c, h, ::-1], rb[0:n, c, ::-1], own[0:n, c, ::-1, 2 + h],
                                    -BIG if first else cr[0:n, c, 1, h:h + 1], ALU.add, ALU.max))
                        k.wait()
                    scans(True)
                    for c, (a, n) in enumerate(CH):
                        k.did(nc.vector.tensor_copy(sm[0:n, c, 0, :], mf[0:n, c, :, P - 1]))
                        k.did(nc.vector.tensor_copy(sm[0:n, c, 1, :], mb[0:n, c, :, 0]))
                        k.did(nc.vector.tensor_reduce(sm[0:n, c, 2, 0:1], rf[0:n, c, :], AX.X, ALU.min))
                        k.did(nc.vector.tensor_reduce(sm[0:n, c, 3, 0:1], rb[0:n, c, :], AX.X, ALU.min))
                    k.wait()
                    for c, (a, n) in enumerate(CH):
                        for q in (2, 3):
                            o = nc.vector.tensor_copy(sm[0:n, c, q, 1:HEADS], sm[0:n, c, q, 0:1].to_broadcast([n, HEADS - 1]))
                            if c < len(CH) - 1 or q == 2:
                                k.did(o)
                    o.then_inc(g_sum, 1)
                    dve.wait_ge(g_rows, 16)
                    nc.vector.tensor_tensor_scan(cs[:, 0, 1:NT + 1], rows[:, 2, :], rows[:, 0, :], -BIG,
                                                 ALU.add, ALU.max).then_inc(g_scan, 1)
                    nc.vector.tensor_tensor_scan(cs[:, 1, NT - 1::-1], rows[:, 3, ::-1], rows[:, 1, ::-1], -BIG,
                                                 ALU.add, ALU.max).then_inc(g_scan, 1)
                    dve.wait_ge(g_car, 32 * len(CH))
                    scans(False)
                    for c, (a, n) in enumerate(CH):
                        k.did(nc.vector.tensor_copy(dwt[0:n, c, :, 0:2].bitcast(i32), own[0:n, c, :, 0:2].bitcast(i32)))
                        k.step(nc.vector.tensor_tensor(dwt[0:n, c, :, 6:10], mf[0:n, c, :, :].rearrange("p h t -> p t h"),
                                                       mb[0:n, c, :, :].rearrange("p h t -> p t h"), ALU.max))
                        nc.vector.tensor_tensor(dwt[0:n, c, :, 2:6], own[0:n, c, :, 2:6], dwt[0:n, c, :, 6:10],
                                                ALU.subtract).then_inc(g_sub, 1)

        ph = ExitStack()
        with ph:
            dw = [alloc(ph, f"dw{s}", [P, G, 12]) for s in range(2)]
            xg = [alloc(ph, f"xg{s}", [P, G, D]) for s in range(2)]
            msg = [alloc(ph, f"msg{s}", [P, G, MW]) for s in range(2)]
            km = [alloc(ph, f"m_key127{s}", [P, G + 1]) for s in range(2)]
            sel = [alloc(ph, f"m_sel{s}", [P, G, P]) for s in range(2)]
            car = [alloc(ph, f"m_car{s}", [P, G, P]) for s in range(2)]
            ct = [alloc(ph, f"ct{s}", [P, G, CW]) for s in range(2)]
            dw_ld, xg_ld, ct_st = sems("m_dw_loaded"), sems("m_x_gathered"), sems("m_ct_stored")
            m_key, m_sel, m_msg, m_sum, m_ct, m_max = (sem("m_key"), sem("m_sel"), sem("m_msg"), sem("m_sum"),
                                                       sem("m_ct"), sem("m_max"))
            m_init, m_ch = sem("m_init"), sem("m_chain")
            with nc.Block() as block:
                @block.sync
                def _(sp):
                    def store(g, s):
                        sp.wait_ge(m_ct, G * (g + 1))
                        sp.wait_ge(m_max, g + 1)
                        sp.dma_start(tiles(CT, g), ct[s][:]).then_inc(ct_st[s], 16)

                    def body(g, s, i, last):
                        need(sp, m_msg, g - 1)
                        need(sp, m_max, g - 1)
                        sp.dma_start(dw[s][:], tiles(DW, g)).then_inc(dw_ld[s], 16)
                        if not early(g, 1):
                            store(g - 1, 1 - s)
                    groups(sp, body)
                    store(GROUPS - 1, 1)
                    for s in range(2):
                        sp.wait_ge(ct_st[s], 16 * PAIRS)

                @block.gpsimd
                def _(pool):
                    def body(g, s, i, last):
                        pool.wait_ge(dw_ld[s], 16 * (i + 1))
                        need(pool, m_msg, g - 1)
                        pool.sem_inc(turn, 1)
                        for j in range(G):
                            pool.indirect_dma_start(
                                out=xg[s][:, j, :], out_offset=None, in_=XP,
                                in_offset=bass.IndirectOffsetOnAxis(ap=dw[s][:, j, 1:2].bitcast(i32), axis=0))\
                                .then_inc(xg_ld[s], 16)
                    groups(pool, body)

                @block.vector
                def _(dve):
                    c = Count(dve, m_ch)
                    for s in range(2):
                        c.did(nc.vector.memset(km[s][:], -1.0))
                    nc.vector.memset(ct[1][:], 0.0).then_inc(m_init, 1)
                    c.wait()
                    base0, STEPS = c.n, 3

                    def body(g, s, i, last):
                        c.at(base0 + g * STEPS)
                        dve.wait_ge(dw_ld[s], 16 * (i + 1))
                        c.did(nc.vector.tensor_scalar(km[s][:, 1:G + 1], dw[s][:, :, 0], is127[:, 0:1], is127[:, 1:2],
                                                      ALU.mult, ALU.add))
                        c.did(nc.vector.tensor_copy(km[s][:, 0:1], km[1 - s][:, G:G + 1]))
                        c.wait()
                        dve.wait_ge(m_key, g + 1)
                        need(dve, m_sum, G * (g - 1))
                        kb = B[s][:].rearrange("p (t n) -> p t n", t=G)
                        c.did(nc.vector.tensor_tensor(sel[s][:], kb, dw[s][:, :, 0:1].to_broadcast([P, G, P]), ALU.is_equal))
                        nc.vector.tensor_tensor(car[s][:], kb, km[s][:, 0:G].unsqueeze(2).to_broadcast([P, G, P]),
                                                ALU.is_equal).then_inc(m_sel, 1)
                        need(dve, ct_st[s], 16 * i)
                        nc.vector.tensor_copy(ct[s][:, :, MW:CW], dw[s][:, :, 6:10]).then_inc(m_max, 1)
                        assert c.n == STEPS
                        dve.wait_ge(xg_ld[s], 16 * G * (i + 1))
                        nc.vector.tensor_copy(msg[s][:, :, D:MW], dw[s][:, :, 2:6])
                        nc.vector.tensor_tensor(msg[s][:, :, 0:D].rearrange("p t (h d) -> p t h d", h=HEADS),
                                                xg[s][:].rearrange("p t (h d) -> p t h d", h=HEADS),
                                                dw[s][:, :, 2:6].unsqueeze(3).to_broadcast([P, G, HEADS, HD]),
                                                ALU.mult).then_inc(m_msg, 1)
                    groups(dve, body)

                @block.tensor
                def _(pe):
                    pe.wait_ge(m_init, 1)

                    def body(g, s, i, last):
                        pe.wait_ge(dw_ld[s], 16 * (i + 1))
                        need(pe, m_sel, g - 1)
                        for j in range(G):
                            o = nc.tensor.transpose(B[s][:, j * P:(j + 1) * P], dw[s][:, j, 0:1].to_broadcast([P, P]),
                                                    ident[:])
                        o.then_inc(m_key, 1)
                        pe.wait_ge(m_sel, g + 1)
                        pe.wait_ge(m_msg, g + 1)
                        for j in range(G):
                            t = g * G + j
                            acc = B[2 + j][:, 0:MW]
                            need(pe, m_ct, t - 3)
                            nc.tensor.matmul(acc, sel[s][:, j, :], msg[s][:, j, :], start=True, stop=False)
                            prev = ct[s][:, j - 1, 0:MW] if j else ct[1 - s][:, G - 1, 0:MW]
                            need(pe, m_ct, t)
                            nc.tensor.matmul(acc, car[s][:, j, :], prev, start=False, stop=True).then_inc(m_sum, 1)
                    groups(pe, body)

                @block.scalar
                def _(act):
                    act.wait_ge(m_init, 1)

                    def body(g, s, i, last):
                        need(act, ct_st[s], 16 * i)
                        for j in range(G):
                            act.wait_ge(m_sum, g * G + j + 1)
                            nc.scalar.copy(ct[s][:, j, 0:MW], B[2 + j][:, 0:MW]).then_inc(m_ct, 1)
                    groups(act, body)

        ph = ExitStack()
        with ph:
            xin = [alloc(ph, f"n_x{s}", [P, G, D]) for s in range(2)]
            xpn = [alloc(ph, f"n_xp{s}", [P, G, D]) for s in range(2)]
            ssn = [alloc(ph, f"n_ss{s}", [P, G, 8]) for s in range(2)]
            cg = [alloc(ph, f"n_cg{s}", [P, G, CW]) for s in range(2)]
            il = [alloc(ph, f"n_last{s}", [P, G], i32) for s in range(2)]
            xb = [alloc(ph, f"n_xb{s}", [P, G, D]) for s in range(2)]
            y = [alloc(ph, f"n_y{s}", [P, G, D]) for s in range(2)]
            x1 = [alloc(ph, f"n_x1{s}", [P, G, D]) for s in range(2)]
            xo = [alloc(ph, f"n_xo{s}", [P, G, D]) for s in range(2)]
            sf = [alloc(ph, f"n_self{s}", [P, G, HEADS]) for s in range(2)]
            mx = [alloc(ph, f"n_max{s}", [P, G, HEADS]) for s in range(2)]
            ea = [alloc(ph, f"n_exp{s}", [P, 2, G, HEADS]) for s in range(2)]
            den = [alloc(ph, f"n_den{s}", [P, G, HEADS]) for s in range(2)]
            st = [[alloc(ph, f"n_stats{k}{s}", [P, G, 6]) for s in range(2)] for k in range(2)]
            mv = [[alloc(ph, f"n_mv{k}{s}", [P, G, 2]) for s in range(2)] for k in range(2)]
            ve = [[alloc(ph, f"n_var{k}{s}", [P, G]) for s in range(2)] for k in range(2)]
            rs = [[alloc(ph, f"n_rstd{k}{s}", [P, G]) for s in range(2)] for k in range(2)]
            nm = [[alloc(ph, f"n_shift{k}{s}", [P, G]) for s in range(2)] for k in range(2)]
            half = alloc(ph, "n_half", [P, G])
            n_ld, n_cg = sems("n_loaded"), sems("n_gathered")
            x1_st, xo_st = sems("n_x1_stored"), sems("n_xo_stored")
            n_half, n_il, n_xb, n_exl, n_exp, n_y = (sem("n_half"), sem("n_il"), sem("n_xb"), sem("n_exl"),
                                                     sem("n_exp"), sem("n_y"))
            n_var = [sem(f"n_var{k}") for k in range(2)]
            n_pow = [sem(f"n_pow{k}") for k in range(2)]
            n_nm = [sem(f"n_nm{k}") for k in range(2)]
            n_stat = [sem(f"n_stat{k}") for k in range(2)]
            n_x1, n_xo, n_ch = sem("n_x1"), sem("n_xo"), sem("n_chain")
            LOADS = 48
            with nc.Block() as block:
                @block.sync
                def _(sp):
                    def body(g, s, i, last):
                        need(sp, n_y, g - 1)
                        need(sp, n_xb, g - 1)
                        load_rows(sp, xin[s], x, g, last, n_ld[s])
                        sp.dma_start(xpn[s][:], tiles(XP, g)).then_inc(n_ld[s], 16)
                        sp.dma_start(ssn[s][:], tiles(SS, g)).then_inc(n_ld[s], 16)
                    groups(sp, body)

                @block.gpsimd
                def _(pool):
                    nc.gpsimd.memset(half[:], -0.5).then_inc(n_half, 1)
                    pool.wait_ge(n_half, 1)

                    def gather(g, s):
                        need(pool, n_y, g - 1)
                        pool.sem_inc(turn, 1)
                        nc.gpsimd.tensor_copy(il[s][:], lastd[:, bass.ds(g * G, G)]).then_inc(n_il, 1)
                        pool.wait_ge(n_il, g + 1)
                        pool.sem_inc(turn, 1)
                        for j in range(G):
                            pool.indirect_dma_start(
                                out=cg[s][:, j, :], out_offset=None, in_=CT,
                                in_offset=bass.IndirectOffsetOnAxis(ap=il[s][:, j:j + 1], axis=0)).then_inc(n_cg[s], 16)

                    def power(k, g, s):
                        pool.wait_ge(n_var[k], g + 1)
                        need(pool, n_nm[k], g - 1)
                        nc.gpsimd.tensor_tensor(rs[k][s][:], ve[k][s][:], half[:], ALU.pow).then_inc(n_pow[k], 1)

                    gather(0, 0)

                    def body(g, s, i, last):
                        if not last:
                            gather(g + 1, 1 - s)
                        pool.wait_ge(n_ld[s], LOADS * (i + 1) + 16 * last)
                        need(pool, n_y, g - 1)
                        nc.gpsimd.tensor_tensor(xb[s][:], xin[s][:], biasb[:].unsqueeze(1).to_broadcast([P, G, D]),
                                                ALU.add).then_inc(n_xb, 1)
                        power(0, g, s)
                        if not early(g, 1):
                            power(1, g - 1, 1 - s)
                    groups(pool, body)
                    power(1, GROUPS - 1, 1)

                @block.vector
                def _(dve):
                    c, STEPS = Count(dve, n_ch), 9
                    cs2 = [Count(dve, n_stat[k]) for k in range(2)]

                    def stats(k, g, s, a):
                        cs2[k].at(g * 2)
                        for j in range(G):
                            o = nc.vector.bn_stats(st[k][s][:, j, :], a[:, j, :])
                        cs2[k].step(o)
                        dve.sem_inc(dturn, 1)
                        for j in range(G):
                            o = nc.vector.bn_aggr(mv[k][s][:, j, :], st[k][s][:, j, :])
                        cs2[k].step(o)
                        nc.vector.tensor_scalar(ve[k][s][:], mv[k][s][:, :, 1], EPS, None, ALU.add).then_inc(n_var[k], 1)

                    def shift(k, g, s):
                        dve.wait_ge(n_pow[k], g + 1)
                        nc.vector.scalar_tensor_tensor(nm[k][s][:], mv[k][s][:, :, 0], -1.0, rs[k][s][:],
                                                       ALU.mult, ALU.mult).then_inc(n_nm[k], 1)

                    def combine(g, s, i, last):
                        c.at(g * STEPS)
                        dve.wait_ge(n_ld[s], LOADS * (i + 1) + 16 * last)
                        c.step(nc.vector.tensor_tensor(sf[s][:], ssn[s][:, :, 0:4], ssn[s][:, :, 4:8], ALU.add))
                        c.step(nc.vector.scalar_tensor_tensor(sf[s][:], sf[s][:], NEG_SLOPE, sf[s][:], ALU.mult, ALU.max))
                        dve.wait_ge(n_cg[s], 16 * G * (i + 1))
                        c.step(nc.vector.tensor_tensor(mx[s][:], sf[s][:], cg[s][:, :, MW:CW], ALU.max))
                        nc.vector.tensor_tensor(ea[s][:, 0], cg[s][:, :, MW:CW], mx[s][:], ALU.subtract)
                        nc.vector.tensor_tensor(ea[s][:, 1], sf[s][:], mx[s][:], ALU.subtract).then_inc(n_exl, 1)
                        dve.wait_ge(n_exp, g + 1)
                        c.step(nc.vector.tensor_tensor(den[s][:], cg[s][:, :, D:MW], ea[s][:, 0], ALU.mult))
                        c.step(nc.vector.scalar_tensor_tensor(den[s][:], den[s][:], 1e-12, ea[s][:, 1], ALU.add, ALU.add))
                        c.step(nc.vector.reciprocal(den[s][:], den[s][:]))
                        nc.vector.tensor_tensor(ea[s][:, 0], ea[s][:, 0], den[s][:], ALU.mult)
                        c.step(nc.vector.tensor_tensor(ea[s][:, 1], ea[s][:, 1], den[s][:], ALU.mult))
                        need(dve, n_x1, g - 1)
                        yh, ch, xh = (a.rearrange("p t (h d) -> p t h d", h=HEADS)
                                      for a in (y[s][:], cg[s][:, :, 0:D], xpn[s][:]))
                        nc.vector.tensor_tensor(yh, ch, ea[s][:, 0].unsqueeze(3).to_broadcast([P, G, HEADS, HD]), ALU.mult)
                        c.step(nc.vector.tensor_tensor(xh, xh, ea[s][:, 1].unsqueeze(3).to_broadcast([P, G, HEADS, HD]),
                                                       ALU.mult))
                        dve.wait_ge(n_xb, g + 1)
                        c.step(nc.vector.tensor_tensor(y[s][:], y[s][:], xpn[s][:], ALU.add))
                        assert c.n == STEPS
                        nc.vector.tensor_tensor(y[s][:], y[s][:], xb[s][:], ALU.add).then_inc(n_y, 1)
                        dve.wait_ge(n_y, g + 1)

                    def second(g, s):
                        dve.wait_ge(n_x1, g + 1)
                        stats(1, g, s, x1[s])

                    def body(g, s, i, last):
                        combine(g, s, i, last)
                        stats(0, g, s, y[s])
                        if not early(g, 1):
                            second(g - 1, 1 - s)
                        shift(0, g, s)
                        if not early(g, 1):
                            shift(1, g - 1, 1 - s)
                    groups(dve, body)
                    second(GROUPS - 1, 1)
                    shift(1, GROUPS - 1, 1)

                @block.scalar
                def _(act):
                    def first_norm(g, s, i):
                        need(act, x1_st[s], 16 * i)
                        act.wait_ge(n_nm[0], g + 1)
                        for j in range(G):
                            o = nc.scalar.activation(x1[s][:, j, :], y[s][:, j, :], ACT.Identity,
                                                     bias=nm[0][s][:, j:j + 1], scale=rs[0][s][:, j:j + 1])
                        o.then_inc(n_x1, 1)
                        act.wait_ge(n_x1, g + 1)
                        act.dma_start(tiles(X1, g), x1[s][:]).then_inc(x1_st[s], 16)

                    def second_norm(g, s, i, last):
                        need(act, xo_st[s], 16 * i)
                        act.wait_ge(n_nm[1], g + 1)
                        for j in range(G):
                            o = nc.scalar.activation(xo[s][:, j, :], x1[s][:, j, :], ACT.Identity,
                                                     bias=nm[1][s][:, j:j + 1], scale=rs[1][s][:, j:j + 1])
                        o.then_inc(n_xo, 1)
                        act.wait_ge(n_xo, g + 1)
                        if not last:
                            act.dma_start(tiles(out, g), xo[s][:]).then_inc(xo_st[s], 16)
                            return
                        act.dma_start(tiles(out, g, TAIL_TILES), xo[s][:, 0:TAIL_TILES, :]).then_inc(xo_st[s], 16)
                        act.dma_start(out[N - TAIL_ROWS:N, :], xo[s][0:TAIL_ROWS, TAIL_TILES, :]).then_inc(xo_st[s], 16)

                    def body(g, s, i, last):
                        act.wait_ge(n_exl, g + 1)
                        nc.scalar.activation(ea[s][:], ea[s][:], ACT.Exp).then_inc(n_exp, 1)
                        first_norm(g, s, i)
                        if not early(g, 1):
                            second_norm(g - 1, 1 - s, i if s == 1 else i - 1, False)
                    groups(act, body)
                    second_norm(GROUPS - 1, 1, PAIRS - 1, True)
                    act.wait_ge(xo_st[0], 16 * PAIRS)
                    act.wait_ge(xo_st[1], 16 * PAIRS + 16)
                    for s in range(2):
                        act.wait_ge(x1_st[s], 16 * PAIRS)

        ph = ExitStack()
        with ph:
            es = [alloc(ph, f"es{s}", [P, G, 4], i32) for s in range(2)]
            nx = [alloc(ph, f"next{s}", [P, G, 1], i32) for s in range(2)]
            ag = [alloc(ph, f"ag{s}", [P, G, D]) for s in range(2)]
            bg = [alloc(ph, f"bg{s}", [P, G, D]) for s in range(2)]
            eg = [alloc(ph, f"eg{s}", [P, G, P]) for s in range(2)]
            ar = [alloc(ph, f"ar{s}", [P, G, D]) for s in range(2)]
            hT = [[alloc(ph, f"hT{s}{k}", [P, 4, G * P], f32r) for k in range(2)] for s in range(2)]
            eT = [[alloc(ph, f"u_eT{s}{k}", [P, G * P], f32r) for k in range(2)] for s in range(2)]
            h1 = [alloc(ph, f"h1{k}", [C0, 4, G * P], f32r) for k in range(2)]
            h2 = [alloc(ph, f"h2{k}", [C1, 3, G * P], f32r) for k in range(2)]
            mg = [[alloc(ph, f"u_msg{s}{k}", [P, G, HW], f32r) for k in range(2)] for s in range(2)]
            th = [alloc(ph, f"tanh{k}", [P, G * P]) for k in range(2)]
            mf = [alloc(ph, f"message{k}", [P, D]) for k in range(2)]
            gs = [alloc(ph, f"gate{k}", [P, D]) for k in range(2)]
            cc = [alloc(ph, f"u_sum{s}", [P, G, HW]) for s in range(2)]
            kf = [alloc(ph, f"u_key{s}", [P, G]) for s in range(2)]
            nf = [alloc(ph, f"u_next{s}", [P, G]) for s in range(2)]
            km = [alloc(ph, f"u_key127{s}", [P, G + 1]) for s in range(2)]
            si = [alloc(ph, f"u_row{s}", [P, G], i32) for s in range(2)]
            sel = alloc(ph, "u_sel", [P, G, P], f32r)
            car = alloc(ph, "u_car", [P, G, P])
            rc = [alloc(ph, f"u_rc{s}", [P, G, 1]) for s in range(2)]
            y = [alloc(ph, f"u_y{s}", [P, G, D]) for s in range(2)]
            st = [alloc(ph, f"u_stats{s}", [P, G, 6]) for s in range(2)]
            mv = [alloc(ph, f"u_mv{s}", [P, G, 2]) for s in range(2)]
            ve = [alloc(ph, f"u_var{s}", [P, G]) for s in range(2)]
            rs = [alloc(ph, f"u_rstd{s}", [P, G]) for s in range(2)]
            nm = [alloc(ph, f"u_shift{s}", [P, G]) for s in range(2)]
            half = alloc(ph, "u_half", [P, G])
            es_ld, gath, o_st = sems("u_es_loaded"), sems("u_gathered"), sems("u_out_stored")
            u_half, u_keys, u_tp, u_td, u_ta = sem("u_half"), sem("u_keys"), sem("u_tp"), sem("u_td"), sem("u_ta")
            u_l, u_h, u_q, u_g, u_m = sem("u_l"), sem("u_h"), sem("u_q"), sem("u_g"), sem("u_m")
            u_kt, u_sel, u_sum, u_cc, u_ar = sem("u_kt"), sem("u_sel"), sem("u_sum"), sem("u_cc"), sem("u_ar")
            u_var, u_pow, u_nm, u_xo, u_si = sem("u_var"), sem("u_pow"), sem("u_nm"), sem("u_xo"), sem("u_si")
            u_init, u_chk, u_chf, u_chs, u_chn, u_y = (sem("u_init"), sem("u_chain_keys"), sem("u_chain_fin"),
                                                       sem("u_chain_sel"), sem("u_chain_row"), sem("u_y"))
            u_hl, u_mf, u_mh = sem("u_hl"), sem("u_mf"), sem("u_mh")
            JOBS = 5
            BL = (2, 3, 4)
            use_bank = [BL[0], BL[1], BL[2], BL[0], BL[1], BL[2], BL[0]]
            prev_use = [6 - 7, 4 - 7, 5 - 7, 0, 1, 2, 3]

            with nc.Block() as block:
                @block.sync
                def _(sp):
                    def load(g, s):
                        need(sp, u_keys, g - 1)
                        sp.dma_start(es[s][:], tiles(ES, g)).then_inc(es_ld[s], 16)
                        with nc.allow_non_contiguous_dma(reason="one key of each row"):
                            sp.dma_start(nx[s][:], shifted(ES, g, 1)[:, :, 0:1]).then_inc(es_ld[s], 16)
                    load(0, 0)
                    load(1, 1)

                    def body(g, s, i, last):
                        if not late(g, 2):
                            sp.wait_ge(gath[s], 48 * G * (i + 1))
                            load(g + 2, s)
                    groups(sp, body)

                @block.gpsimd
                def _(pool):
                    nc.gpsimd.memset(half[:], -0.5).then_inc(u_half, 1)
                    pool.wait_ge(u_half, 1)

                    def gather(g, s, i):
                        pool.wait_ge(es_ld[s], 32 * (i + 1))
                        need(pool, u_tp, JOBS * (g - 1))
                        need(pool, u_ar, g - 1)
                        pool.sem_inc(turn, 1)
                        for j in range(G):
                            for k, (buf, table) in enumerate(((ag, X1), (bg, X1), (eg, e128))):
                                pool.indirect_dma_start(
                                    out=buf[s][:, j, :], out_offset=None, in_=table,
                                    in_offset=bass.IndirectOffsetOnAxis(ap=es[s][:, j, k:k + 1], axis=0))\
                                    .then_inc(gath[s], 16)

                    def scatter(g, s):
                        pool.wait_ge(u_xo, g + 1)
                        pool.wait_ge(u_si, g + 1)
                        pool.sem_inc(turn, 1)
                        for j in range(G):
                            pool.indirect_dma_start(
                                out=out, out_offset=bass.IndirectOffsetOnAxis(ap=si[s][:, j:j + 1], axis=0),
                                in_=y[s][:, j, :], in_offset=None, bounds_check=N - 1, oob_is_err=False)\
                                .then_inc(o_st[s], 16)

                    def power(g, s):
                        pool.wait_ge(u_var, g + 1)
                        need(pool, u_nm, g - 1)
                        need(pool, u_xo, g - 1)
                        nc.gpsimd.tensor_tensor(rs[s][:], ve[s][:], half[:], ALU.pow).then_inc(u_pow, 1)
                    gather(0, 0, 0)
                    gather(1, 1, 0)

                    def body(g, s, i, last):
                        if not late(g, 2):
                            gather(g + 2, s, i + 1)
                        if not early(g, 2):
                            scatter(g - 2, s)
                        if not early(g, 1):
                            power(g - 1, 1 - s)
                    groups(pool, body)
                    scatter(GROUPS - 2, 0)
                    power(GROUPS - 1, 1)
                    scatter(GROUPS - 1, 1)
                    for s in range(2):
                        pool.wait_ge(o_st[s], 16 * G * PAIRS)

                @block.tensor
                def _(pe):
                    pe.wait_ge(u_init, 1)

                    def transposes(g, s, i, k):
                        if k == 0:
                            pe.wait_ge(gath[s], 48 * G * (i + 1))
                        need(pe, u_td, JOBS * g + (k - 1 if k >= 2 else (0, -1)[k]))
                        if k == 1:
                            need(pe, u_sel, g - 1)
                        for j in range(G):
                            a = (ag, ag, bg, bg)[k][s][:, j, (k % 2) * P:(k % 2) * P + P] if k < 4 else eg[s][:, j, :]
                            o = nc.tensor.transpose(B[k % 2][:, j * P:(j + 1) * P], a, ident[:])
                        o.then_inc(u_tp, 1)

                    def product(acc, terms, ready=None):
                        n = 3 * len(terms)
                        for k, (a, b) in enumerate(terms):
                            if ready is not None:
                                pe.wait_ge(u_hl, ready + k)
                            for p, q in ((0, 0), (0, 1), (1, 0)):
                                n -= 1
                                o = nc.tensor.matmul(acc, a[p], b[q], start=(n == 3 * len(terms) - 1), stop=(n == 0))
                        return o

                    def combine(g, s, j):
                        t = g * G + j
                        need(pe, u_cc, t)
                        if j == 0:
                            pe.wait_ge(u_sel, g + 1)
                            pe.wait_ge(u_m, (g + 1) * G)
                        acc = B[7][:, 0:HW]
                        prev = cc[s][:, j - 1, :] if j else cc[1 - s][:, G - 1, :]
                        for k in range(2):
                            nc.tensor.matmul(acc, sel[:, j, :], mg[s][k][:, j, :], start=(k == 0), stop=False)
                        nc.tensor.matmul(acc, car[:, j, :], prev, start=False, stop=True).then_inc(u_sum, 1)

                    def body(g, s, i, last):
                        for m, (a, n) in enumerate(M0):
                            if m == 0:
                                pe.wait_ge(u_td, JOBS * (g + 1))
                            need(pe, u_h, 7 * g + prev_use[m] + 1)
                            o = product(B[use_bank[m]][0:n, :],
                                        [((w0r[0][:, k, a:a + n], w0r[1][:, k, a:a + n]), (hT[s][0][:, k, :], hT[s][1][:, k, :]))
                                         for k in range(4)])
                            o.then_inc(u_l, 1)
                            if not late(g, 1):
                                transposes(g + 1, 1 - s, i if s == 0 else i + 1, m)
                        for m, (a, n) in enumerate(M1):
                            need(pe, u_h, 7 * g + prev_use[4 + m] + 1)
                            o = product(B[use_bank[4 + m]][0:n, :],
                                        [((w1r[0][0:kn, k, a:a + n], w1r[1][0:kn, k, a:a + n]),
                                          (h1[0][0:kn, k, :], h1[1][0:kn, k, :])) for k, (_, kn) in enumerate(M0)],
                                        ready=7 * g + 1 if m == 0 else None)
                            o.then_inc(u_l, 1)
                            if m == 0 and not late(g, 1):
                                transposes(g + 1, 1 - s, i if s == 0 else i + 1, 4)
                        for j in range(G):
                            if not early(g, 1):
                                combine(g - 1, 1 - s, j)
                            t = g * G + j
                            need(pe, u_mf, t - 1)
                            e = slice(j * P, (j + 1) * P)
                            rows_of = [kn + (k == 2) for k, (_, kn) in enumerate(M1)]
                            product(B[5 + j % 2][:, D:2 * D],
                                    [((eT[s][0][:, e], eT[s][1][:, e]), (wgr[0][:], wgr[1][:]))])
                            product(B[5 + j % 2][:, 0:D],
                                    [((h2[0][0:kn, k, e], h2[1][0:kn, k, e]), (w2r[0][0:kn, k, :], w2r[1][0:kn, k, :]))
                                     for k, kn in enumerate(rows_of)], ready=7 * g + 5 if j == 0 else None).then_inc(u_q, 1)
                        need(pe, u_td, JOBS * (g + 1 if late(g, 1) else g + 2))
                        pe.wait_ge(u_keys, g + 1)
                        for j in range(G):
                            o = nc.tensor.transpose(B[1][:, j * P:(j + 1) * P], kf[s][:, j:j + 1].to_broadcast([P, P]), ident[:])
                        o.then_inc(u_kt, 1)
                    for k in range(JOBS):
                        transposes(0, 0, 0, k)
                    groups(pe, body)
                    for j in range(G):
                        combine(GROUPS - 1, 1, j)

                @block.scalar
                def _(act):
                    def evac(g, s, k):
                        act.wait_ge(u_tp, JOBS * g + k + 1)
                        nc.scalar.copy(hT[s][0][:, k, :] if k < 4 else eT[s][0][:], B[k % 2][:]).then_inc(u_ta, 1)

                    def keep(g, s, i):
                        act.wait_ge(gath[s], 48 * G * (i + 1))
                        need(act, u_y, g - 1)
                        nc.scalar.copy(ar[s][:], ag[s][:]).then_inc(u_ar, 1)

                    def norm(g, s, i):
                        act.wait_ge(u_nm, g + 1)
                        need(act, o_st[s], 16 * G * i)
                        for j in range(G):
                            o = nc.scalar.activation(y[s][:, j, :], y[s][:, j, :], ACT.Identity,
                                                     bias=nm[s][:, j:j + 1], scale=rs[s][:, j:j + 1])
                        o.then_inc(u_xo, 1)

                    def high_message(g, s, j):
                        act.wait_ge(u_mf, g * G + j + 1)
                        need(act, u_sum, G * (g - 1))
                        nc.scalar.copy(mg[s][0][:, j, 0:D], mf[j % 2][:]).then_inc(u_mh, 1)

                    def hidden(use, b, acc, high, bias, n, again=0):
                        act.wait_ge(u_l, use + 1)
                        need(act, u_hl, use - 1 + again)
                        nc.scalar.activation(th[b][0:n, :], acc, ACT.Tanh, bias=bias)
                        nc.scalar.activation(high, acc, ACT.Tanh, bias=bias).then_inc(u_h, 1)

                    def body(g, s, i, last):
                        for m, (a, n) in enumerate(M0):
                            hidden(7 * g + m, m % 2, B[use_bank[m]][0:n, :], h1[0][0:n, m, :], b0s[0:n, m:m + 1], n,
                                   again=(m == 0))
                            if not late(g, 1):
                                evac(g + 1, 1 - s, m)
                        for m, (a, n) in enumerate(M1):
                            hidden(7 * g + 4 + m, m % 2, B[use_bank[4 + m]][0:n, :], h2[0][0:n, m, :], b1s[0:n, m:m + 1], n)
                            if m == 0 and not late(g, 1):
                                evac(g + 1, 1 - s, 4)
                        for j in range(G):
                            t = g * G + j
                            act.wait_ge(u_q, t + 1)
                            need(act, u_mf, t - 1)
                            nc.scalar.copy(gs[j % 2][:], B[5 + j % 2][:, D:2 * D]).then_inc(u_g, 1)
                            if j:
                                high_message(g, s, j - 1)
                        high_message(g, s, G - 1)
                        if not early(g, 2):
                            norm(g - 2, s, i - 1)
                        if not late(g, 1):
                            keep(g + 1, 1 - s, i if s == 0 else i + 1)
                    act.wait_ge(u_init, 1)
                    for k in range(JOBS):
                        evac(0, 0, k)
                    keep(0, 0, 0)
                    groups(act, body)
                    norm(GROUPS - 2, 0, PAIRS - 1)
                    norm(GROUPS - 1, 1, PAIRS - 1)

                @block.vector
                def _(dve):
                    ck, cf, cs_, cn = Count(dve, u_chk), Count(dve, u_chf), Count(dve, u_chs), Count(dve, u_chn)
                    for s in range(2):
                        ck.did(nc.vector.memset(km[s][:], -1.0))
                        ck.did(nc.vector.memset(mg[s][0][:, :, D:D + 1].bitcast(f32), 1.0))
                        ck.did(nc.vector.memset(mg[s][0][:, :, D + 1:HW].bitcast(f32), 0.0))
                        ck.did(nc.vector.memset(mg[s][1][:, :, D:HW].bitcast(f32), 0.0))
                    ck.did(nc.vector.memset(h2[0][:, 2, :].bitcast(f32), 1.0))
                    ck.did(nc.vector.memset(h2[1][:, 2, :].bitcast(f32), 0.0))
                    nc.vector.memset(cc[1][:], 0.0).then_inc(u_init, 1)
                    ck.wait()
                    base0 = ck.n

                    def evac(g, s, k):
                        dve.wait_ge(u_ta, JOBS * g + k + 1)
                        hi, lo = (hT[s][q][:, k, :] if k < 4 else eT[s][q][:] for q in range(2))
                        nc.vector.tensor_tensor(lo, B[k % 2][:], hi.bitcast(f32), ALU.subtract).then_inc(u_td, 1)

                    def low_message(g, s, j):
                        dve.wait_ge(u_mh, g * G + j + 1)
                        nc.vector.tensor_tensor(mg[s][1][:, j, 0:D], mf[j % 2][:], mg[s][0][:, j, 0:D].bitcast(f32),
                                                ALU.subtract).then_inc(u_m, 1)

                    def low(use, h, m, n):
                        dve.wait_ge(u_h, use + 1)
                        nc.vector.tensor_tensor(h[1][0:n, m, :], th[m % 2][0:n, :], h[0][0:n, m, :].bitcast(f32),
                                                ALU.subtract).then_inc(u_hl, 1)

                    def keys(g, s, i):
                        ck.at(base0 + g * 2)
                        dve.wait_ge(es_ld[s], 32 * (i + 1))
                        ck.did(nc.vector.tensor_copy(nf[s][:], nx[s][:, :, 0]))
                        nc.vector.tensor_copy(kf[s][:], es[s][:, :, 0]).then_inc(u_keys, 1)
                        dve.wait_ge(u_keys, g + 1)
                        nc.vector.tensor_scalar(km[s][:, 1:G + 1], kf[s][:], is127[:, 0:1], is127[:, 1:2],
                                                ALU.mult, ALU.add)
                        ck.step(nc.vector.tensor_copy(km[s][:, 0:1], km[1 - s][:, G:G + 1]))

                    def row_index(g, s, i):
                        need(dve, o_st[s], 16 * G * i)
                        cn.at(g)
                        cn.step(nc.vector.tensor_tensor(nf[s][:], kf[s][:], nf[s][:], ALU.is_equal))
                        nc.vector.scalar_tensor_tensor(si[s][:], nf[s][:], OOB, kf[s][:], ALU.mult, ALU.add)\
                            .then_inc(u_si, 1)

                    def finish(g, s, i):
                        cf.at(g * 3)
                        cf.step(nc.vector.reciprocal(rc[s][:], cc[s][:, :, D:D + 1]))
                        need(dve, u_xo, g - 1)
                        dve.wait_ge(u_ar, g + 1)
                        for j in range(G):
                            o = nc.vector.scalar_tensor_tensor(y[s][:, j, :], cc[s][:, j, 0:D], rc[s][:, j, :],
                                                               ar[s][:, j, :], ALU.mult, ALU.add)
                        o.then_inc(u_y, 1)
                        dve.wait_ge(u_y, g + 1)
                        for j in range(G):
                            o = nc.vector.bn_stats(st[s][:, j, :], y[s][:, j, :])
                        cf.step(o)
                        dve.sem_inc(dturn, 1)
                        for j in range(G):
                            o = nc.vector.bn_aggr(mv[s][:, j, :], st[s][:, j, :])
                        cf.step(o)
                        nc.vector.tensor_scalar(ve[s][:], mv[s][:, :, 1], EPS, None, ALU.add).then_inc(u_var, 1)

                    def shift(g, s):
                        dve.wait_ge(u_pow, g + 1)
                        nc.vector.scalar_tensor_tensor(nm[s][:], mv[s][:, :, 0], -1.0, rs[s][:],
                                                       ALU.mult, ALU.mult).then_inc(u_nm, 1)

                    def sums(g, s, j):
                        dve.wait_ge(u_sum, g * G + j + 1)
                        nc.vector.tensor_copy(cc[s][:, j, :], B[7][:, 0:HW]).then_inc(u_cc, 1)
                        if j == G - 1:
                            dve.wait_ge(u_cc, (g + 1) * G)

                    def body(g, s, i, last):
                        if not early(g, 2):
                            shift(g - 2, s)
                        keys(g, s, i)
                        for m, (a, n) in enumerate(M0):
                            low(7 * g + m, h1, m, n)
                            if not late(g, 1):
                                evac(g + 1, 1 - s, m)
                        for m, (a, n) in enumerate(M1):
                            low(7 * g + 4 + m, h2, m, n)
                            if m == 0 and not late(g, 1):
                                evac(g + 1, 1 - s, 4)
                        for j in range(G):
                            if not early(g, 1):
                                sums(g - 1, 1 - s, j)
                            dve.wait_ge(u_g, g * G + j + 1)
                            need(dve, u_m, g * G + j - 1)
                            nc.vector.tensor_tensor(mf[j % 2][:], B[5 + j % 2][:, 0:D], gs[j % 2][:],
                                                    ALU.mult).then_inc(u_mf, 1)
                            if j:
                                low_message(g, s, j - 1)
                        low_message(g, s, G - 1)
                        dve.wait_ge(u_kt, g + 1)
                        kb = B[1][:].rearrange("p (t n) -> p t n", t=G)
                        nc.vector.tensor_tensor(sel[:], kb, kf[s][:].unsqueeze(2).to_broadcast([P, G, P]), ALU.is_equal)
                        nc.vector.tensor_tensor(car[:], kb, km[s][:, 0:G].unsqueeze(2).to_broadcast([P, G, P]),
                                                ALU.is_equal).then_inc(u_sel, 1)
                        if not early(g, 1):
                            k = i if s == 1 else i - 1
                            row_index(g - 1, 1 - s, k)
                            finish(g - 1, 1 - s, k)
                    dve.wait_ge(u_init, 1)
                    for k in range(JOBS):
                        evac(0, 0, k)
                    groups(dve, body)
                    shift(GROUPS - 2, 0)
                    for j in range(G):
                        sums(GROUPS - 1, 1, j)
                    row_index(GROUPS - 1, 1, PAIRS - 1)
                    finish(GROUPS - 1, 1, PAIRS - 1)
                    shift(GROUPS - 1, 1)

_INS = ['x', 'src', 'dst', 'edge_attr_128', 'edge_attr_32', 'L0_gnn_lin_W', 'L0_gnn_att_src', 'L0_gnn_att_dst',
        'L0_gnn_lin_edge_W', 'L0_gnn_att_edge', 'L0_gnn_bias', 'L1_gnn_W0', 'L1_gnn_b0', 'L1_gnn_W1',
        'L1_gnn_b1', 'L1_gnn_W2', 'L1_gnn_b2', 'L1_gnn_Wg']


def kernel(**inputs):
    import concourse.bacc as bacc
    import numpy as np
    from concourse.bass_utils import run_bass_kernel_spmd

    nc = bacc.Bacc("TRN2", target_bir_lowering=False, num_devices=1)
    arrays, args = {}, []
    for name in _INS:
        a = np.ascontiguousarray(inputs[name])
        arrays[f"in_{name}"] = a
        args.append(nc.dram_tensor(f"in_{name}", a.shape, mybir.dt.from_np(a.dtype), kind="ExternalInput").ap())
    shape = tuple(inputs['x'].shape)
    args.append(nc.dram_tensor("out_x", shape, mybir.dt.float32, kind="ExternalOutput").ap())
    gnn_kernel(nc, *args)
    r = run_bass_kernel_spmd(nc, [arrays], core_ids=[0])
    return r.results[0]["out_x"]
```

```python
from contextlib import ExitStack

import concourse.bass as bass
from concourse import mybir

P = 128
G = 4
HEADS = 4
NEG_SLOPE = 0.2
EPS = 1e-5
BIG = 3e38


class Count:

    def __init__(self, eng, sem):
        self.eng, self.sem, self.base, self.n = eng, sem, 0, 0

    def at(self, base):
        self.base, self.n = base, 0

    def did(self, ins):
        self.n += 1
        ins.then_inc(self.sem, 1)

    def wait(self):
        self.eng.wait_ge(self.sem, self.base + self.n)

    def step(self, ins):
        self.did(ins)
        self.wait()


def pieces(total, size):
    return [(a, min(size, total - a)) for a in range(0, total, size)]


def gnn_kernel(nc, x, src, dst, e128, e32, lin_W, att_src, att_dst, lin_edge_W, att_edge, bias,
               W0, b0, W1, b1, W2, b2, Wg, out):
    f32, f16, i32, f32r = mybir.dt.float32, mybir.dt.float16, mybir.dt.int32, mybir.dt.float32r
    ALU, ACT, AX = mybir.AluOpType, mybir.ActivationFunctionType, mybir.AxisListType

    N, D = x.shape
    HD = D // HEADS
    KE = e32.shape[1]
    GROUPS = N // (G * P) + 1
    NT = G * GROUPS
    NP = NT * P
    PAIRS = GROUPS // 2
    PEEL = 2
    assert GROUPS % 2 == 0 and D == 2 * P and KE * G == P and e128.shape[1] == P
    TAIL_TILES, TAIL_ROWS = divmod(N - (GROUPS - 1) * G * P, P)
    F0, F1 = W0.shape[1], W1.shape[1]
    C1 = -(-F1 // 3)
    M0, M1 = pieces(F0, P), pieces(F1, C1)
    A0, R0 = M0[-1]
    STACK = (0, 32, 64)
    T0 = STACK[-1] + R0
    assert len(M0) == 4 and R0 <= 32 and R0 % 2 == 0
    assert M1[-1][1] < C1
    XW = D + 2 * HEADS
    MW = D + HEADS
    CW = D + 2 * HEADS
    HW = D + 2
    OOB = 2.0 ** 20

    XP = nc.dram_tensor("XP", (NP, D), f32, kind="Internal").ap()
    SS = nc.dram_tensor("SS", (NP, 8), f32, kind="Internal").ap()
    DS = nc.dram_tensor("DS", (NP + 2, 8), f32, kind="Internal").ap()
    ES = nc.dram_tensor("ES", (NP + 1, 4), i32, kind="Internal").ap()
    VS = nc.dram_tensor("VS", (4, HEADS, NT), f32, kind="Internal").ap()
    CS = nc.dram_tensor("CS", (2, HEADS, NT + 1), f32, kind="Internal").ap()
    DW = nc.dram_tensor("DW", (NP, 12), f32, kind="Internal").ap()
    CT = nc.dram_tensor("CT", (NP + 1, CW), f32, kind="Internal").ap()
    X1 = nc.dram_tensor("X1", (NP, D), f32, kind="Internal").ap()

    def tiles(a, g, n=G):
        return a[bass.ds(g * (G * P), n * P), :].rearrange("(t p) w -> p t w", p=P)

    def shifted(a, g, by):
        return a[bass.ds(g * (G * P) + by, G * P), :].rearrange("(t p) w -> p t w", p=P)

    def groups(eng, body):
        for g in range(2 * PEEL):
            body(g, g % 2, g // 2, False)
        with eng.Fori(PEEL, PAIRS - 1) as i:
            for s in range(2):
                body(i * 2 + s, s, i, False)
        for s in range(2):
            body(2 * PAIRS - 2 + s, s, PAIRS - 1, s == 1)

    def need(eng, sem, n):
        if not (isinstance(n, int) and n <= 0):
            eng.wait_ge(sem, n)

    def early(g, n):
        return isinstance(g, int) and g < n

    def late(g, n):
        return isinstance(g, int) and g + n >= GROUPS

    def load_rows(eng, buf, a, g, last, sem):
        if not last:
            eng.dma_start(buf[:, :, :], tiles(a, g)).then_inc(sem, 16)
            return
        eng.dma_start(buf[:, 0:TAIL_TILES, :], tiles(a, g, TAIL_TILES)).then_inc(sem, 16)
        r0 = N - TAIL_ROWS
        eng.dma_start(buf[0:TAIL_ROWS, TAIL_TILES, :], a[r0:N, :]).then_inc(sem, 16)

    top = ExitStack()
    with top:
        def alloc(stack, name, shape, dt=f32):
            return stack.enter_context(nc.sbuf_tensor(name, shape, dt))

        def sem(name):
            return top.enter_context(nc.semaphore(name))

        def sems(name, n=2):
            return [sem(f"{name}{i}") for i in range(n)]

        turn = sem("pool_turn")
        dturn = sem("dve_turn")

        B = [top.enter_context(nc.psum_tensor(f"bank{i}", [P, 512], f32)) for i in range(8)]

        ident = alloc(top, "ident", [P, P])
        identh = alloc(top, "identh", [P, P], f16)
        ones = alloc(top, "ones", [P, P])
        before = alloc(top, "before", [P, P])
        after = alloc(top, "after", [P, P])
        iota = alloc(top, "iota", [P, max(NT, P)], f16)
        is127 = alloc(top, "is127", [P, 2])
        wst = alloc(top, "wst", [P, 2, XW])
        wedge = alloc(top, "wedge", [P, 4 * HEADS])
        biasb = alloc(top, "biasb", [P, D])
        w0r = [alloc(top, f"w0r{k}", [P, 4, F0], f32r) for k in range(2)]
        w0t = [alloc(top, f"w0t{k}", [P, 4, T0], f32r) for k in range(2)]
        w1r = [alloc(top, f"w1r{k}", [P, 3, F1], f32r) for k in range(2)]
        w1t = alloc(top, "w1t", [T0, F1], f32r)
        w2r = [alloc(top, f"w2r{k}", [C1, 3, D], f32r) for k in range(2)]
        wgr = [alloc(top, f"wgr{k}", [P, D], f32r) for k in range(2)]
        b0s = alloc(top, "b0s", [P, 4])
        b1s = alloc(top, "b1s", [C1, 3])
        lastd = alloc(top, "lastd", [P, NT], i32)

        ph = ExitStack()
        with ph:
            lw = alloc(ph, "lw", [P, 2, D])
            w0s = alloc(ph, "w0s", [P, 4, F0])
            w1s = alloc(ph, "w1s", [P, 3, F1])
            w1ts = alloc(ph, "w1ts", [T0, F1])
            w2s = alloc(ph, "w2s", [C1, 3, D])
            wgs = alloc(ph, "wgs", [P, D])
            le4 = alloc(ph, "le4", [P, 2, 4, KE])
            ab = alloc(ph, "ab", [P, 2, 3 * HEADS])
            ioi = alloc(ph, "ioi", [P, max(NT, P)], i32)
            s_zero, s_load, s_const = sem("w_zero"), sem("w_load"), sem("w_const")
            s_attl, s_mm, s_ev = sem("w_att"), sem("w_mm"), sem("w_ev")
            with nc.Block() as block:
                @block.gpsimd
                def _(pool):
                    c = Count(pool, s_const)
                    c.did(nc.gpsimd.memset(ident[:], 0.0))
                    c.did(nc.gpsimd.memset(ones[:], 1.0))
                    c.did(nc.gpsimd.memset(before[:], 1.0))
                    c.did(nc.gpsimd.memset(after[:], 1.0))
                    c.did(nc.gpsimd.memset(is127[:, 0:1], 0.0))
                    c.did(nc.gpsimd.memset(is127[:, 1:2], -1.0))
                    c.did(nc.gpsimd.iota(ioi[:], pattern=[[1, max(NT, P)]], base=0, channel_multiplier=0))
                    c.wait()
                    c.did(nc.gpsimd.affine_select(out=ident[:], in_=ident[:], compare_op=ALU.not_equal,
                                                  fill=1.0, base=0, pattern=[[-1, P]], channel_multiplier=1))
                    c.did(nc.gpsimd.affine_select(out=before[:], in_=before[:], compare_op=ALU.is_gt,
                                                  fill=0.0, base=0, pattern=[[-1, P]], channel_multiplier=1))
                    c.did(nc.gpsimd.affine_select(out=after[:], in_=after[:], compare_op=ALU.is_gt,
                                                  fill=0.0, base=0, pattern=[[1, P]], channel_multiplier=-1))
                    for k in range(2):
                        c.did(nc.gpsimd.affine_select(out=is127[:, k:k + 1], in_=is127[:, k:k + 1],
                                                      compare_op=ALU.not_equal, fill=1.0 - k, base=1 - P,
                                                      pattern=[[0, 1]], channel_multiplier=1))
                    c.did(nc.gpsimd.tensor_copy(iota[:], ioi[:]))
                    c.wait()
                    c.did(nc.gpsimd.tensor_copy(identh[:], ident[:]))

                @block.sync
                def _(sp):
                    sp.wait_ge(s_zero, 1)
                    with nc.allow_non_contiguous_dma(reason="small weight vectors"):
                        for k, a in enumerate((att_src, att_dst, att_edge)):
                            for h in range(HEADS):
                                r = (h % 2) * HD
                                sp.dma_start(ab[r:r + HD, h // 2, k * HEADS + h:k * HEADS + h + 1],
                                             a[h, :].rearrange("(d a) -> d a", a=1)).then_inc(s_attl, 16)
                        for r, k, a, n in [(0, k, a, n) for k, (a, n) in enumerate(M0[:3])] + \
                                          [(r, 3, A0, R0) for r in STACK]:
                            sp.dma_start(b0s[r:r + n, k:k + 1], b0[a:a + n].rearrange("(d a) -> d a", a=1))\
                                .then_inc(s_load, 16)
                        for k, (a, n) in enumerate(M1):
                            sp.dma_start(b1s[0:n, k:k + 1], b1[a:a + n].rearrange("(d a) -> d a", a=1))\
                                .then_inc(s_load, 16)
                    sp.wait_ge(s_load, 16 * 9)

                @block.scalar
                def _(act):
                    act.dma_start(lw[:], lin_W.rearrange("(c p) i -> p c i", p=P)).then_inc(s_attl, 16)
                    for r in range(4):
                        act.dma_start(le4[:, :, r, :], lin_edge_W.rearrange("(c p) k -> p c k", p=P))\
                            .then_inc(s_attl, 16)
                    act.dma_start(biasb[:], bias.partition_broadcast(P)).then_inc(s_attl, 16)
                    act.dma_start(w0s[:], W0.rearrange("(c p) m -> p c m", p=P)).then_inc(s_attl, 16)
                    for k, (a, n) in enumerate(M0[:3]):
                        act.dma_start(w1s[0:n, k, :], W1[a:a + n, :]).then_inc(s_attl, 16)
                    act.wait_ge(s_zero, 1)
                    for r in STACK:
                        act.dma_start(w1ts[r:r + R0, :], W1[A0:F0, :]).then_inc(s_attl, 16)
                    for k, (a, n) in enumerate(M1):
                        act.dma_start(w2s[0:n, k, :], W2[a:a + n, :]).then_inc(s_attl, 16)
                    a, n = M1[-1]
                    act.dma_start(w2s[n:n + 1, 2, :], b2.rearrange("(a d) -> a d", a=1)).then_inc(s_attl, 16)
                    act.dma_start(wgs[:], Wg).then_inc(s_attl, 16)
                    act.wait_ge(s_attl, 16 * (3 * HEADS + 18))

                @block.vector
                def _(dve):
                    nc.vector.memset(w1ts[:], 0.0)
                    nc.vector.memset(b0s[:], 0.0)
                    nc.vector.memset(ab[:], 0.0).then_inc(s_zero, 1)
                    c = Count(dve, s_ev)
                    for k in range(2):
                        c.did(nc.vector.memset(w0t[k][:].bitcast(f32), 0.0))
                    c.wait()
                    c.did(nc.vector.memset(wedge[:], 0.0))
                    dve.wait_ge(s_attl, 16 * (3 * HEADS + 18))
                    parts = [(w0r, w0s, P, slice(0, 4)), (wgr, wgs, P, None)]
                    parts += [(w1r, w1s, n, k) for k, (a, n) in enumerate(M0[:3])]
                    parts += [(w2r, w2s, n + (k == 2), k) for k, (a, n) in enumerate(M1)]
                    for low in range(2):
                        for w, full, n, k in parts:
                            hi, lo, f = (t[0:n] if k is None else t[0:n, k, :] for t in (w[0], w[1], full))
                            if low:
                                c.did(nc.vector.tensor_tensor(lo, f, hi.bitcast(f32), ALU.subtract))
                            else:
                                c.did(nc.vector.tensor_copy(hi, f))
                        for r in STACK:
                            t, f = [w[:, :, r:r + R0] for w in w0t], w0s[:, :, A0:F0]
                            if low:
                                c.did(nc.vector.tensor_tensor(t[1], f, t[0].bitcast(f32), ALU.subtract))
                            else:
                                c.did(nc.vector.tensor_copy(t[0], f))
                        r = slice(STACK[1], STACK[1] + R0)
                        if low:
                            c.did(nc.vector.tensor_tensor(w1t[r], w1ts[r], w1t[r].bitcast(f32), ALU.subtract))
                        else:
                            c.did(nc.vector.tensor_copy(w1t[:], w1ts[:]))
                        c.wait()
                    dve.wait_ge(s_mm, 1)
                    for k in range(2):
                        c.did(nc.vector.tensor_copy(wst[:, k, 0:D], B[k][:, 0:D]))
                    dve.wait_ge(s_mm, 2)
                    for k in range(2):
                        c.did(nc.vector.tensor_copy(wst[:, k, D:XW], B[2 + k][:, 0:8]))
                    c.wait()
                    for r in range(4):
                        c.did(nc.vector.tensor_copy(wedge[r * KE:(r + 1) * KE, r * HEADS:(r + 1) * HEADS],
                                                    B[4][r * KE:(r + 1) * KE, 0:HEADS]))

                @block.tensor
                def _(pe):
                    pe.wait_ge(s_const, 12)
                    pe.wait_ge(s_attl, 16 * (3 * HEADS + 18))
                    for k in range(2):
                        for c in range(2):
                            t = nc.tensor.transpose(B[k][:, c * P:(c + 1) * P], lw[:, c, k * P:(k + 1) * P], ident[:])
                    t.then_inc(s_mm, 1)
                    for k in range(2):
                        for c in range(2):
                            nc.tensor.matmul(B[2 + k][:, 0:8], lw[:, c, k * P:(k + 1) * P], ab[:, c, 0:8],
                                             start=(c == 0), stop=(c == 1))
                    for c in range(2):
                        t = nc.tensor.matmul(B[4][:, 0:HEADS], le4[:, c, :, :].rearrange("p r k -> p (r k)"),
                                             ab[:, c, 8:12], start=(c == 0), stop=(c == 1))
                    t.then_inc(s_mm, 1)

        ph = ExitStack()
        with ph:
            xin = [alloc(ph, f"xin{s}", [P, G, D]) for s in range(2)]
            xT = [alloc(ph, f"xT{s}", [P, 2, G * P]) for s in range(2)]
            xps = [alloc(ph, f"xps{s}", [P, G, XW]) for s in range(2)]
            x_loaded, xp_stored = sems("p_x_loaded"), sems("p_xp_stored")
            xt_psum, xt_d, xt_a = sem("p_xt_psum"), sem("p_xt_dve"), sem("p_xt_act")
            pr_psum, pr_d, pr_a = sem("p_pr_psum"), sem("p_pr_dve"), sem("p_pr_act")
            with nc.Block() as block:
                @block.sync
                def _(sp):
                    def body(g, s, i, last):
                        need(sp, xt_psum, 2 * (g - 1))
                        load_rows(sp, xin[s], x, g, last, x_loaded[s])
                    groups(sp, body)

                @block.tensor
                def _(pe):
                    def transposes(g, s, i, last):
                        pe.wait_ge(x_loaded[s], 16 * (i + 1) + 16 * last)
                        need(pe, xt_d, g - 1)
                        need(pe, xt_a, g - 1)
                        for k in range(2):
                            for j in range(G):
                                t = nc.tensor.transpose(B[2 * s + k][:, j * P:(j + 1) * P],
                                                        xin[s][:, j, k * P:(k + 1) * P], ident[:])
                            t.then_inc(xt_psum, 1)

                    def body(g, s, i, last):
                        if not late(g, 1):
                            transposes(g + 1, 1 - s, i if s == 0 else i + 1, late(g, 2))
                        pe.wait_ge(xt_d, g + 1)
                        pe.wait_ge(xt_a, g + 1)
                        for j in range(G):
                            need(pe, (pr_d, pr_a)[j % 2], 2 * g + j // 2 - 1)
                            for k in range(2):
                                t = nc.tensor.matmul(B[4 + j][:, 0:XW], xT[s][:, k, j * P:(j + 1) * P], wst[:, k, :],
                                                     start=(k == 0), stop=(k == 1))
                            t.then_inc(pr_psum, 1)
                    transposes(0, 0, 0, False)
                    groups(pe, body)

                @block.vector
                def _(dve):
                    def half(g, s):
                        need(dve, pr_psum, 4 * (g - 1))
                        dve.wait_ge(xt_psum, 2 * g + 1)
                        nc.vector.tensor_copy(xT[s][:, 0, :], B[2 * s][:]).then_inc(xt_d, 1)

                    def body(g, s, i, last):
                        if not late(g, 1):
                            half(g + 1, 1 - s)
                        need(dve, xp_stored[s], 32 * i)
                        for j in (0, 2):
                            dve.wait_ge(pr_psum, 4 * g + j + 1)
                            nc.vector.tensor_copy(xps[s][:, j, :], B[4 + j][:, 0:XW]).then_inc(pr_d, 1)
                    half(0, 0)
                    groups(dve, body)

                @block.scalar
                def _(act):
                    def half(g, s):
                        need(act, pr_psum, 4 * (g - 1))
                        act.wait_ge(xt_psum, 2 * g + 2)
                        nc.scalar.copy(xT[s][:, 1, :], B[2 * s + 1][:]).then_inc(xt_a, 1)

                    def body(g, s, i, last):
                        if not late(g, 1):
                            half(g + 1, 1 - s)
                        need(act, xp_stored[s], 32 * i)
                        for j in (1, 3):
                            act.wait_ge(pr_psum, 4 * g + j + 1)
                            nc.scalar.copy(xps[s][:, j, :], B[4 + j][:, 0:XW]).then_inc(pr_a, 1)
                    half(0, 0)
                    groups(act, body)

                @block.gpsimd
                def _(pool):
                    def body(g, s, i, last):
                        pool.wait_ge(pr_d, 2 * g + 2)
                        pool.wait_ge(pr_a, 2 * g + 2)
                        pool.sem_inc(turn, 1)
                        pool.dma_start(tiles(XP, g), xps[s][:, :, 0:D]).then_inc(xp_stored[s], 16)
                        pool.dma_start(tiles(SS, g), xps[s][:, :, D:XW]).then_inc(xp_stored[s], 16)
                    groups(pool, body)
                    for s in range(2):
                        pool.wait_ge(xp_stored[s], 32 * PAIRS)
        NC = -(-NT // P)
        srt = ExitStack()
        with srt:
            keys = (dst, src)
            KI = [alloc(srt, f"key_int{q}", [P, NT], i32) for q in range(2)]
            KF = [alloc(srt, f"key{q}", [P, NT]) for q in range(2)]
            LO = [alloc(srt, f"key_lo{q}", [P, NT]) for q in range(2)]
            HI = [alloc(srt, f"key_hi{q}", [P, NT]) for q in range(2)]
            start = [alloc(srt, f"start{q}", [P, NT]) for q in range(2)]
            eid = alloc(srt, "eid", [P, NT], i32)
            ssrc = alloc(srt, "ssrc", [P, NT, HEADS])
            ohlo = [[alloc(srt, f"ohlo{q}{s}", [P, G, P], f16) for s in range(2)] for q in range(2)]
            ohhi = [[alloc(srt, f"ohhi{q}{s}", [P, G, NT], f16) for s in range(2)] for q in range(2)]

            def one_hots(g, s, j, done):
                t = bass.ds(g * G + j, 1)
                for q in range(2):
                    nc.vector.tensor_scalar(ohlo[q][s][:, j, :], iota[:, 0:P], LO[q][:, t], None, ALU.is_equal)
                    o = nc.vector.tensor_scalar(ohhi[q][s][:, j, :], iota[:, 0:NT], HI[q][:, t], None, ALU.is_equal)
                if j == G - 1:
                    o.then_inc(done, 1)

            ph = ExitStack()
            with ph:
                kr = [alloc(ph, f"key_rows{q}", [P, NC, P], i32) for q in range(2)]
                krf = [alloc(ph, f"key_rowsf{q}", [P, NC, P]) for q in range(2)]
                ki = [alloc(ph, f"key_digit{q}", [P, NT], i32) for q in range(4)]
                hist = [alloc(ph, f"hist{q}", [P, NT]) for q in range(2)]
                tot = [alloc(ph, f"tot{q}", [P, NT]) for q in range(2)]
                cum = [alloc(ph, f"cum{q}", [P, NT]) for q in range(2)]
                eid0 = alloc(ph, "eid0", [P, NT], i32)
                sent = alloc(ph, "sentinel", [1, 8])
                senti = alloc(ph, "sentinel_int", [1, 4], i32)
                ix = [alloc(ph, f"h_src{s}", [P, G], i32) for s in range(2)]
                sg = [alloc(ph, f"h_sgather{s}", [P, G, 8]) for s in range(2)]
                h_sg, h_ix, h_res = sems("h_s_gathered"), sem("h_ix"), sem("h_sg_copied")
                h_pad, h_loaded, h_rows, h_psum = sem("h_pad"), sem("h_loaded"), sem("h_rows"), sem("h_psum")
                h_chain, h_oh, h_acc, h_hist, h_sums = sem("h_chain"), sem("h_oh"), sem("h_acc"), sem("h_hist"), sem("h_sums")
                fr, rr = divmod(N, P)
                loads = [(c, min(P, fr - c * P)) for c in range(NC) if fr - c * P > 0]
                with nc.Block() as block:
                    @block.gpsimd
                    def _(pool):
                        for q in range(2):
                            nc.gpsimd.memset(kr[q][:], N).then_inc(h_pad, 1)
                        nc.gpsimd.memset(sent[:], -1.0).then_inc(h_pad, 1)
                        nc.gpsimd.memset(senti[:], -1).then_inc(h_pad, 1)
                        nc.gpsimd.iota(eid0[:], pattern=[[P, NT]], base=0, channel_multiplier=1).then_inc(h_pad, 1)

                        def body(g, s, i, last):
                            pool.wait_ge(h_ix, g + 1)
                            need(pool, h_res, g - 1)
                            pool.sem_inc(turn, 1)
                            for j in range(G):
                                pool.indirect_dma_start(
                                    out=sg[s][:, j, :], out_offset=None, in_=SS,
                                    in_offset=bass.IndirectOffsetOnAxis(ap=ix[s][:, j:j + 1], axis=0))\
                                    .then_inc(h_sg[s], 16)
                        groups(pool, body)

                    @block.sync
                    def _(sp):
                        sp.wait_ge(h_pad, 4)
                        for q in range(2):
                            for c, n in loads:
                                sp.dma_start(kr[q][0:n, c, :], keys[q][c * P * P:(c * P + n) * P]
                                             .rearrange("(t p) -> t p", p=P)).then_inc(h_loaded, 16)
                            sp.dma_start(kr[q][fr % P:fr % P + 1, fr // P, 0:rr],
                                         keys[q][fr * P:N].rearrange("(a p) -> a p", a=1)).then_inc(h_loaded, 16)
                        sp.dma_start(DS[0:1, :], sent[:]).then_inc(h_loaded, 16)
                        sp.dma_start(DS[NP + 1:NP + 2, :], sent[:]).then_inc(h_loaded, 16)
                        sp.dma_start(ES[NP:NP + 1, :], senti[:]).then_inc(h_loaded, 16)
                        sp.wait_ge(h_loaded, 16 * (2 * len(loads) + 5))

                    @block.vector
                    def _(dve):
                        c = Count(dve, h_chain)
                        dve.wait_ge(h_loaded, 16 * (2 * len(loads) + 5))
                        for q in range(2):
                            nc.vector.tensor_copy(krf[q][:], kr[q][:]).then_inc(h_rows, 1)
                        dve.wait_ge(h_pad, 5)
                        c.did(nc.vector.tensor_scalar(eid[:], eid0[:], N - 1, None, ALU.min))
                        dve.wait_ge(h_psum, 1)
                        for q in range(2):
                            c.did(nc.vector.tensor_copy(KF[q][:], B[q][:, 0:NT]))
                            c.did(nc.vector.tensor_copy(KI[q][:], B[q][:, 0:NT]))
                        c.wait()
                        for q in range(2):
                            c.did(nc.vector.tensor_scalar(ki[q][:], KI[q][:], P - 1, None, ALU.bitwise_and))
                            c.did(nc.vector.tensor_scalar(ki[2 + q][:], KI[q][:], 7, None, ALU.arith_shift_right))
                        c.wait()
                        for q in range(2):
                            c.did(nc.vector.tensor_copy(LO[q][:], ki[q][:]))
                            c.did(nc.vector.tensor_copy(HI[q][:], ki[2 + q][:]))
                        c.wait()

                        def keep(g, s, i):
                            dve.wait_ge(h_sg[s], 16 * G * (i + 1))
                            nc.vector.tensor_copy(ssrc[:, bass.ds(g * G, G), :], sg[s][:, :, 0:HEADS]).then_inc(h_res, 1)

                        def body(g, s, i, last):
                            if not early(g, 2):
                                keep(g - 2, s, i - 1)
                            nc.vector.tensor_copy(ix[s][:], KI[1][:, bass.ds(g * G, G)]).then_inc(h_ix, 1)
                            need(dve, h_acc, g - 1)
                            for j in range(G):
                                one_hots(g, s, j, h_oh)
                        groups(dve, body)
                        for s in range(2):
                            keep(GROUPS - 2 + s, s, PAIRS - 1)
                        dve.wait_ge(h_acc, GROUPS)
                        for q in range(2):
                            nc.vector.tensor_copy(hist[q][:], B[q][:, 0:NT]).then_inc(h_hist, 1)
                        dve.wait_ge(h_sums, 1)
                        for q in range(2):
                            c.did(nc.vector.tensor_copy(tot[q][:], B[2 + q][:, 0:NT]))
                        c.wait()
                        for q in range(2):
                            c.did(nc.vector.tensor_tensor_scan(cum[q][:], tot[q][:], tot[q][:], 0.0, ALU.add, ALU.max))
                        c.wait()
                        for q in range(2):
                            c.did(nc.vector.tensor_tensor(cum[q][:], cum[q][:], tot[q][:], ALU.subtract))
                        c.wait()
                        for q in range(2):
                            c.did(nc.vector.tensor_tensor(start[q][:], cum[q][:], B[4 + q][:, 0:NT], ALU.add))
                        c.wait()
                        c.step(nc.vector.scalar_tensor_tensor(tot[0][:], start[0][:], -1.0 - NP, hist[0][:],
                                                              ALU.add, ALU.add))
                        c.step(nc.vector.scalar_tensor_tensor(tot[1][:], hist[0][:], 0.0, tot[0][:],
                                                              ALU.is_gt, ALU.mult))
                        c.did(nc.vector.tensor_scalar(lastd[:], tot[1][:], float(NP), None, ALU.add))

                    @block.tensor
                    def _(pe):
                        pe.wait_ge(h_rows, 2)
                        for q in range(2):
                            for c in range(NC):
                                t = nc.tensor.transpose(B[q][:, c * P:(c + 1) * P], krf[q][:, c, :], ident[:])
                        t.then_inc(h_psum, 1)

                        def body(g, s, i, last):
                            pe.wait_ge(h_oh, g + 1)
                            for q in range(2):
                                for j in range(G):
                                    first = isinstance(g, int) and g == 0 and j == 0
                                    t = nc.tensor.matmul(B[q][:, 0:NT], ohlo[q][s][:, j, :], ohhi[q][s][:, j, :],
                                                         start=first, stop=last and j == G - 1)
                            t.then_inc(h_acc, 1)
                        groups(pe, body)
                        pe.wait_ge(h_hist, 2)
                        for q in range(2):
                            nc.tensor.matmul(B[2 + q][:, 0:NT], ones[:], hist[q][:], start=True, stop=True)
                            t = nc.tensor.matmul(B[4 + q][:, 0:NT], after[:], hist[q][:], start=True, stop=True)
                        t.then_inc(h_sums, 1)

            ph = ExitStack()
            with ph:
                tab = [[alloc(ph, f"table{q}{k}", [P, NT]) for k in range(2)] for q in range(2)]
                oT = [alloc(ph, f"ohloT{k}", [P, 2, P]) for k in range(2)]
                oh_psum = B[3][:, 0:P].bitcast(f16)
                kb = (2, 7)
                eqj = [alloc(ph, f"eq{q}", [P, P]) for q in range(2)]
                lkj = [alloc(ph, f"found{q}", [P, NT]) for q in range(2)]
                cnt = [[alloc(ph, f"earlier{q}{s}", [P, G]) for s in range(2)] for q in range(2)]
                rk = [[alloc(ph, f"rank{q}{s}", [P, G]) for s in range(2)] for q in range(2)]
                ri = [[alloc(ph, f"rank_int{q}{s}", [P, G], i32) for s in range(2)] for q in range(2)]
                kcol = [[alloc(ph, f"key_col{q}{s}", [P, G]) for s in range(2)] for q in range(2)]
                ix = [alloc(ph, f"r_dst{s}", [P, G], i32) for s in range(2)]
                sg = [alloc(ph, f"r_sgather{s}", [P, G, 8]) for s in range(2)]
                pd = [alloc(ph, f"by_dst{s}", [P, G, 8]) for s in range(2)]
                pp = [alloc(ph, f"by_src{s}", [P, G, 4], i32) for s in range(2)]
                lg = [alloc(ph, f"logit{s}", [P, G, HEADS]) for s in range(2)]
                ein = [alloc(ph, f"ein{s}", [P, G, KE]) for s in range(2)]
                eT = [alloc(ph, f"eT{s}", [P, P]) for s in range(2)]
                e_ld, sg_ld = sems("r_e_loaded"), sems("r_s_gathered")
                ds_st, es_st = sems("r_ds_stored"), sems("r_es_stored")
                r_init, r_oh, r_ix, r_tk, r_upd = sem("r_init"), sem("r_oh"), sem("r_ix"), sem("r_tk"), sem("r_upd")
                r_ott = sem("r_ott")
                r_look, r_ot, r_tab, r_eq, r_rank = sem("r_look"), sem("r_ot"), sem("r_tab"), sem("r_eq"), sem("r_rank")
                r_et, r_eta, r_ae, r_pay, r_ch = sem("r_et"), sem("r_et_act"), sem("r_ae"), sem("r_pay"), sem("r_chain")
                with nc.Block() as block:
                    @block.sync
                    def _(sp):
                        def body(g, s, i, last):
                            need(sp, r_et, g - 1)
                            load_rows(sp, ein[s], e32, g, last, e_ld[s])
                        groups(sp, body)

                    @block.gpsimd
                    def _(pool):
                        def scatters(g, s):
                            pool.wait_ge(r_pay, g + 1)
                            pool.sem_inc(turn, 1)
                            for j in range(G):
                                pool.indirect_dma_start(
                                    out=DS, out_offset=bass.IndirectOffsetOnAxis(ap=ri[0][s][:, j:j + 1], axis=0),
                                    in_=pd[s][:, j, :], in_offset=None).then_inc(ds_st[s], 16)
                                pool.indirect_dma_start(
                                    out=ES, out_offset=bass.IndirectOffsetOnAxis(ap=ri[1][s][:, j:j + 1], axis=0),
                                    in_=pp[s][:, j, :], in_offset=None).then_inc(es_st[s], 16)

                        def body(g, s, i, last):
                            pool.wait_ge(r_ix, g + 1)
                            pool.sem_inc(turn, 1)
                            for j in range(G):
                                pool.indirect_dma_start(
                                    out=sg[s][:, j, :], out_offset=None, in_=SS,
                                    in_offset=bass.IndirectOffsetOnAxis(ap=ix[s][:, j:j + 1], axis=0))\
                                    .then_inc(sg_ld[s], 16)
                            if not early(g, 1):
                                scatters(g - 1, 1 - s)
                        groups(pool, body)
                        scatters(GROUPS - 1, 1)
                        for s in range(2):
                            pool.wait_ge(ds_st[s], 16 * G * PAIRS)
                            pool.wait_ge(es_st[s], 16 * G * PAIRS)

                    @block.scalar
                    def _(act):
                        def body(g, s, i, last):
                            for j in range(G):
                                t, b = g * G + j, j % 2
                                for q in range(2):
                                    if isinstance(t, int) and t == 0:
                                        act.wait_ge(r_init, 1)
                                    need(act, r_upd, 2 * t + q - 1)
                                    need(act, r_look, 2 * (t - 1) + q - 1)
                                    nc.scalar.copy(tab[q][b][:], B[q][:, 0:NT]).then_inc(r_tab, 1)
                                act.wait_ge(r_ott, t + 1)
                                nc.scalar.copy(oT[b][:].rearrange("p q n -> p (q n)"), oh_psum).then_inc(r_ot, 1)
                            act.wait_ge(r_et, g + 1)
                            nc.scalar.copy(eT[s][:], B[6][:, 0:P]).then_inc(r_eta, 1)
                        groups(act, body)

                    @block.tensor
                    def _(pe):
                        for q in range(2):
                            t = nc.tensor.matmul(B[q][:, 0:NT], ident[:], start[q][:], start=True, stop=True)
                        t.then_inc(r_init, 1)

                        def body(g, s, i, last):
                            pe.wait_ge(r_oh, g + 1)
                            for j in range(G):
                                t, b = g * G + j, j % 2
                                need(pe, r_ot, t)
                                for q in range(2):
                                    o = nc.tensor.transpose(oh_psum[:, q * P:(q + 1) * P], ohlo[q][s][:, j, :],
                                                            identh[:])
                                o.then_inc(r_ott, 1)
                                need(pe, r_eq, 2 * (t - 1))
                                for q in range(2):
                                    o = nc.tensor.transpose(B[kb[b]][:, q * P:(q + 1) * P],
                                                            kcol[q][s][:, j:j + 1].to_broadcast([P, P]), ident[:])
                                o.then_inc(r_tk, 1)
                                for q in range(2):
                                    pe.wait_ge(r_tab, 2 * t + q + 1)
                                    nc.tensor.matmul(B[q][:, 0:NT], ohlo[q][s][:, j, :], ohhi[q][s][:, j, :],
                                                     start=False, stop=True,
                                                     skip_group_check=True).then_inc(r_upd, 1)
                                for q in range(2):
                                    pe.wait_ge(r_ot, t + 1)
                                    need(pe, r_rank, 2 * (t - 1) + q + 1)
                                    nc.tensor.matmul(B[4 + q][:, 0:NT], oT[b][:, q, :], tab[q][b][:],
                                                     start=True, stop=True).then_inc(r_look, 1)
                            pe.wait_ge(e_ld[s], 16 * (i + 1) + 16 * last)
                            need(pe, r_pay, g)
                            nc.tensor.transpose(B[6][:, 0:P], ein[s][:, :, :].rearrange("p t k -> p (t k)"), ident[:])\
                                .then_inc(r_et, 1)
                            pe.wait_ge(r_eta, g + 1)
                            nc.tensor.matmul(B[6][:, 256:256 + G * HEADS], eT[s][:], wedge[:],
                                             start=True, stop=True).then_inc(r_ae, 1)
                        groups(pe, body)

                    @block.vector
                    def _(dve):
                        c = Count(dve, r_ch)
                        for s in range(2):
                            c.did(nc.vector.memset(pd[s][:], 0.0))
                            c.did(nc.vector.memset(pp[s][:], 0))

                        def keys(g, s):
                            t4 = bass.ds(g * G, G)
                            need(dve, r_look, 8 * (g - 1))
                            for q in range(2):
                                c.did(nc.vector.tensor_copy(kcol[q][s][:], KF[q][:, t4]))
                            nc.vector.tensor_copy(ix[s][:], KI[0][:, t4]).then_inc(r_ix, 1)

                        keys(0, 0)
                        for j in range(G):
                            one_hots(0, 0, j, r_oh)
                        c.wait()
                        base0, STEPS = c.n, 11

                        def body(g, s, i, last):
                            c.at(base0 + g * STEPS)
                            t4 = bass.ds(g * G, G)
                            if not late(g, 1):
                                keys(g + 1, 1 - s)
                            for j in range(G):
                                t = g * G + j
                                for q in range(2):
                                    dve.wait_ge(r_tk, t + 1)
                                    nc.vector.scalar_tensor_tensor(eqj[q][:], B[kb[j % 2]][:, q * P:(q + 1) * P], kcol[q][s][:, j:j + 1],
                                                                   before[:], ALU.is_equal, ALU.mult,
                                                                   accum_out=cnt[q][s][:, j:j + 1]).then_inc(r_eq, 1)
                                if not late(g, 1):
                                    one_hots(g + 1, 1 - s, j, r_oh)
                                for q in range(2):
                                    dve.wait_ge(r_look, 2 * t + q + 1)
                                    dve.wait_ge(r_eq, 2 * t + q + 1)
                                    nc.vector.tensor_tensor_reduce(
                                        out=lkj[q][:], in0=B[4 + q][:, 0:NT], in1=ohhi[q][s][:, j, :], scale=1.0,
                                        scalar=cnt[q][s][:, j:j + 1], op0=ALU.mult, op1=ALU.add,
                                        accum_out=rk[q][s][:, j:j + 1]).then_inc(r_rank, 1)
                            need(dve, ds_st[s], 16 * G * i)
                            need(dve, es_st[s], 16 * G * i)
                            dve.wait_ge(r_rank, 8 * (g + 1))
                            c.did(nc.vector.tensor_scalar(ri[0][s][:], rk[0][s][:], 1.0, None, ALU.add))
                            c.did(nc.vector.tensor_copy(ri[1][s][:], rk[1][s][:]))
                            c.did(nc.vector.tensor_copy(pp[s][:, :, 0], KI[1][:, t4]))
                            c.did(nc.vector.tensor_copy(pp[s][:, :, 1], KI[0][:, t4]))
                            c.did(nc.vector.tensor_copy(pp[s][:, :, 2], eid[:, t4]))
                            c.did(nc.vector.tensor_copy(pd[s][:, :, 0], KF[0][:, t4]))
                            c.did(nc.vector.tensor_copy(pd[s][:, :, 1].bitcast(i32), KI[1][:, t4]))
                            dve.wait_ge(sg_ld[s], 16 * G * (i + 1))
                            c.step(nc.vector.tensor_tensor(lg[s][:], sg[s][:, :, HEADS:8], ssrc[:, t4, :], ALU.add))
                            dve.wait_ge(r_ae, g + 1)
                            c.step(nc.vector.tensor_tensor(
                                lg[s][:], lg[s][:], B[6][:, 256:256 + G * HEADS].rearrange("p (t h) -> p t h", t=G), ALU.add))
                            assert c.n == STEPS or late(g, 1)
                            nc.vector.scalar_tensor_tensor(pd[s][:, :, 2:6], lg[s][:], NEG_SLOPE, lg[s][:],
                                                           ALU.mult, ALU.max).then_inc(r_pay, 1)
                        groups(dve, body)
        CH = pieces(NT, P)
        ph = ExitStack()
        with ph:
            own = alloc(ph, "own", [P, NC, P, 8])
            prv = alloc(ph, "prv", [P, NC, P, 8])
            nxt = alloc(ph, "nxt", [P, NC, P, 8])
            rf = alloc(ph, "reset_f", [P, NC, P])
            rb = alloc(ph, "reset_b", [P, NC, P])
            mf = alloc(ph, "max_f", [P, NC, HEADS, P])
            mb = alloc(ph, "max_b", [P, NC, HEADS, P])
            sm = alloc(ph, "row_sums", [P, NC, 4, HEADS])
            cr = alloc(ph, "carry", [P, NC, 2, HEADS])
            rows = alloc(ph, "rows", [HEADS, 4, NT])
            cs = alloc(ph, "carries", [HEADS, 2, NT + 1])
            dwt = alloc(ph, "dwt", [P, NC, P, 12])
            dummy = alloc(ph, "no_edges", [1, CW])
            g_ld, g_sum, g_rows, g_scan = sem("g_loaded"), sem("g_summary"), sem("g_rows"), sem("g_scan")
            g_cst, g_car, g_sub, g_exp, g_st = sem("g_cs_stored"), sem("g_carry"), sem("g_sub"), sem("g_exp"), sem("g_stored")
            g_vst, g_ch = sem("g_vs_stored"), sem("g_chain")
            with nc.Block() as block:
                @block.sync
                def _(sp):
                    for c, (a, n) in enumerate(CH):
                        for k, buf in ((1, own), (0, prv), (2, nxt)):
                            sp.dma_start(buf[0:n, c, :, :].rearrange("p t w -> p (t w)"),
                                         DS[a * P + k:(a + n) * P + k, :].rearrange("(p t) w -> p (t w)", t=P))\
                                .then_inc(g_ld, 16)
                    sp.wait_ge(g_sum, 1)
                    with nc.allow_non_contiguous_dma(reason="row summaries, once"):
                        for c, (a, n) in enumerate(CH):
                            for k in range(4):
                                sp.dma_start(VS[k, :, a:a + n].rearrange("h t -> t h"), sm[0:n, c, k, :]).then_inc(g_vst, 16)
                        sp.wait_ge(g_vst, 64 * len(CH))
                        sp.dma_start(rows[:], VS.rearrange("k h t -> h k t")).then_inc(g_rows, 16)
                        sp.wait_ge(g_scan, 2)
                        sp.dma_start(CS.rearrange("k h t -> h k t"), cs[:]).then_inc(g_cst, 16)
                        sp.wait_ge(g_cst, 16)
                        for c, (a, n) in enumerate(CH):
                            for k in range(2):
                                sp.dma_start(cr[0:n, c, k, :], CS[k, :, a + k:a + k + n].rearrange("h t -> t h"))\
                                    .then_inc(g_car, 16)
                    for c, (a, n) in enumerate(CH):
                        sp.wait_ge(g_exp, c + 1)
                        sp.dma_start(DW[a * P:(a + n) * P, :].rearrange("(p t) w -> p (t w)", t=P),
                                     dwt[0:n, c, :, :].rearrange("p t w -> p (t w)")).then_inc(g_st, 16)
                    sp.dma_start(CT[NP:NP + 1, :], dummy[:]).then_inc(g_st, 16)
                    sp.wait_ge(g_st, 16 * (len(CH) + 1))

                @block.scalar
                def _(act):
                    for c, (a, n) in enumerate(CH):
                        act.wait_ge(g_sub, c + 1)
                        nc.scalar.activation(dwt[0:n, c, :, 2:6], dwt[0:n, c, :, 2:6], ACT.Exp).then_inc(g_exp, 1)

                @block.vector
                def _(dve):
                    k = Count(dve, g_ch)
                    k.did(nc.vector.memset(dwt[:], 0.0))
                    k.did(nc.vector.memset(cs[:], -BIG))
                    k.did(nc.vector.memset(dummy[:, 0:MW], 0.0))
                    k.did(nc.vector.memset(dummy[:, MW:CW], -1e30))
                    dve.wait_ge(g_ld, 48 * len(CH))
                    for c, (a, n) in enumerate(CH):
                        k.did(nc.vector.tensor_tensor(rf[0:n, c, :], own[0:n, c, :, 0], prv[0:n, c, :, 0], ALU.not_equal))
                        k.did(nc.vector.tensor_tensor(rb[0:n, c, :], own[0:n, c, :, 0], nxt[0:n, c, :, 0], ALU.not_equal))
                    k.wait()
                    for c, (a, n) in enumerate(CH):
                        k.did(nc.vector.tensor_scalar(rf[0:n, c, :], rf[0:n, c, :], -BIG, None, ALU.mult))
                        k.did(nc.vector.tensor_scalar(rb[0:n, c, :], rb[0:n, c, :], -BIG, None, ALU.mult))
                    k.wait()

                    def scans(first):
                        for c, (a, n) in enumerate(CH):
                            for h in range(HEADS):
                                k.did(nc.vector.tensor_tensor_scan(
                                    mf[0:n, c, h, :], rf[0:n, c, :], own[0:n, c, :, 2 + h],
                                    -BIG if first else cr[0:n, c, 0, h:h + 1], ALU.add, ALU.max))
                                k.did(nc.vector.tensor_tensor_scan(
                                    mb[0:n, c, h, ::-1], rb[0:n, c, ::-1], own[0:n, c, ::-1, 2 + h],
                                    -BIG if first else cr[0:n, c, 1, h:h + 1], ALU.add, ALU.max))
                        k.wait()
                    scans(True)
                    for c, (a, n) in enumerate(CH):
                        k.did(nc.vector.tensor_copy(sm[0:n, c, 0, :], mf[0:n, c, :, P - 1]))
                        k.did(nc.vector.tensor_copy(sm[0:n, c, 1, :], mb[0:n, c, :, 0]))
                        k.did(nc.vector.tensor_reduce(sm[0:n, c, 2, 0:1], rf[0:n, c, :], AX.X, ALU.min))
                        k.did(nc.vector.tensor_reduce(sm[0:n, c, 3, 0:1], rb[0:n, c, :], AX.X, ALU.min))
                    k.wait()
                    for c, (a, n) in enumerate(CH):
                        for q in (2, 3):
                            o = nc.vector.tensor_copy(sm[0:n, c, q, 1:HEADS], sm[0:n, c, q, 0:1].to_broadcast([n, HEADS - 1]))
                            if c < len(CH) - 1 or q == 2:
                                k.did(o)
                    o.then_inc(g_sum, 1)
                    dve.wait_ge(g_rows, 16)
                    nc.vector.tensor_tensor_scan(cs[:, 0, 1:NT + 1], rows[:, 2, :], rows[:, 0, :], -BIG,
                                                 ALU.add, ALU.max).then_inc(g_scan, 1)
                    nc.vector.tensor_tensor_scan(cs[:, 1, NT - 1::-1], rows[:, 3, ::-1], rows[:, 1, ::-1], -BIG,
                                                 ALU.add, ALU.max).then_inc(g_scan, 1)
                    dve.wait_ge(g_car, 32 * len(CH))
                    scans(False)
                    for c, (a, n) in enumerate(CH):
                        k.did(nc.vector.tensor_copy(dwt[0:n, c, :, 0:2].bitcast(i32), own[0:n, c, :, 0:2].bitcast(i32)))
                        k.step(nc.vector.tensor_tensor(dwt[0:n, c, :, 6:10], mf[0:n, c, :, :].rearrange("p h t -> p t h"),
                                                       mb[0:n, c, :, :].rearrange("p h t -> p t h"), ALU.max))
                        nc.vector.tensor_tensor(dwt[0:n, c, :, 2:6], own[0:n, c, :, 2:6], dwt[0:n, c, :, 6:10],
                                                ALU.subtract).then_inc(g_sub, 1)

        ph = ExitStack()
        with ph:
            dw = [alloc(ph, f"dw{s}", [P, G, 12]) for s in range(2)]
            sr = [alloc(ph, f"m_src{s}", [P, G, 1]) for s in range(2)]
            xg = [alloc(ph, f"xg{s}", [P, G, D]) for s in range(2)]
            msg = [alloc(ph, f"msg{s}", [P, G, MW]) for s in range(2)]
            km = [alloc(ph, f"m_key127{s}", [P, G + 1]) for s in range(2)]
            sel = [alloc(ph, f"m_sel{s}", [P, G, P]) for s in range(2)]
            car = [alloc(ph, f"m_car{s}", [P, G, P]) for s in range(2)]
            ct = [alloc(ph, f"ct{s}", [P, G, CW]) for s in range(2)]
            sr_ld, dw_ld, xg_ld, ct_st = sems("m_src_loaded"), sems("m_dw_loaded"), sems("m_x_gathered"), sems("m_ct_stored")
            m_key, m_sel, m_msg, m_sum, m_ct, m_max = (sem("m_key"), sem("m_sel"), sem("m_msg"), sem("m_sum"),
                                                       sem("m_ct"), sem("m_max"))
            m_init, m_ch = sem("m_init"), sem("m_chain")
            with nc.Block() as block:
                @block.sync
                def _(sp):
                    def sources(g, s):
                        with nc.allow_non_contiguous_dma(reason="one word of each row"):
                            sp.dma_start(sr[s][:], tiles(DW, g)[:, :, 1:2]).then_inc(sr_ld[s], 16)

                    sources(0, 0)
                    sources(1, 1)

                    def body(g, s, i, last):
                        need(sp, m_msg, g - 1)
                        need(sp, m_max, g - 1)
                        sp.dma_start(dw[s][:], tiles(DW, g)).then_inc(dw_ld[s], 16)
                        if not late(g, 2):
                            sp.wait_ge(xg_ld[s], 16 * G * (i + 1))
                            sources(g + 2, s)
                    groups(sp, body)

                @block.gpsimd
                def _(pool):
                    def body(g, s, i, last):
                        pool.wait_ge(sr_ld[s], 16 * (i + 1))
                        need(pool, m_msg, g - 1)
                        pool.sem_inc(turn, 1)
                        for j in range(G):
                            pool.indirect_dma_start(
                                out=xg[s][:, j, :], out_offset=None, in_=XP,
                                in_offset=bass.IndirectOffsetOnAxis(ap=sr[s][:, j, :].bitcast(i32), axis=0))\
                                .then_inc(xg_ld[s], 16)
                    groups(pool, body)

                @block.vector
                def _(dve):
                    c = Count(dve, m_ch)
                    for s in range(2):
                        c.did(nc.vector.memset(km[s][:], -1.0))
                    nc.vector.memset(ct[1][:], 0.0).then_inc(m_init, 1)
                    c.wait()
                    base0, STEPS = c.n, 3

                    def body(g, s, i, last):
                        c.at(base0 + g * STEPS)
                        dve.wait_ge(dw_ld[s], 16 * (i + 1))
                        c.did(nc.vector.tensor_scalar(km[s][:, 1:G + 1], dw[s][:, :, 0], is127[:, 0:1], is127[:, 1:2],
                                                      ALU.mult, ALU.add))
                        c.did(nc.vector.tensor_copy(km[s][:, 0:1], km[1 - s][:, G:G + 1]))
                        c.wait()
                        dve.wait_ge(m_key, g + 1)
                        need(dve, m_sum, G * (g - 1))
                        kb = B[s][:].rearrange("p (t n) -> p t n", t=G)
                        c.did(nc.vector.tensor_tensor(sel[s][:], kb, dw[s][:, :, 0:1].to_broadcast([P, G, P]), ALU.is_equal))
                        nc.vector.tensor_tensor(car[s][:], kb, km[s][:, 0:G].unsqueeze(2).to_broadcast([P, G, P]),
                                                ALU.is_equal).then_inc(m_sel, 1)
                        need(dve, ct_st[s], 16 * i)
                        nc.vector.tensor_copy(ct[s][:, :, MW:CW], dw[s][:, :, 6:10]).then_inc(m_max, 1)
                        assert c.n == STEPS
                        dve.wait_ge(xg_ld[s], 16 * G * (i + 1))
                        nc.vector.tensor_copy(msg[s][:, :, D:MW], dw[s][:, :, 2:6])
                        nc.vector.tensor_tensor(msg[s][:, :, 0:D].rearrange("p t (h d) -> p t h d", h=HEADS),
                                                xg[s][:].rearrange("p t (h d) -> p t h d", h=HEADS),
                                                dw[s][:, :, 2:6].unsqueeze(3).to_broadcast([P, G, HEADS, HD]),
                                                ALU.mult).then_inc(m_msg, 1)
                    groups(dve, body)

                @block.tensor
                def _(pe):
                    pe.wait_ge(m_init, 1)

                    def keys(g, s, i):
                        pe.wait_ge(dw_ld[s], 16 * (i + 1))
                        need(pe, m_sel, g - 1)
                        for j in range(G):
                            o = nc.tensor.transpose(B[s][:, j * P:(j + 1) * P], dw[s][:, j, 0:1].to_broadcast([P, P]),
                                                    ident[:])
                        o.then_inc(m_key, 1)

                    def body(g, s, i, last):
                        if not late(g, 1):
                            keys(g + 1, 1 - s, i if s == 0 else i + 1)
                        pe.wait_ge(m_sel, g + 1)
                        pe.wait_ge(m_msg, g + 1)
                        for j in range(G):
                            t = g * G + j
                            acc = B[2 + j][:, 0:MW]
                            need(pe, m_ct, t - 3)
                            nc.tensor.matmul(acc, sel[s][:, j, :], msg[s][:, j, :], start=True, stop=False)
                            prev = ct[s][:, j - 1, 0:MW] if j else ct[1 - s][:, G - 1, 0:MW]
                            need(pe, m_ct, t)
                            nc.tensor.matmul(acc, car[s][:, j, :], prev, start=False, stop=True).then_inc(m_sum, 1)
                    keys(0, 0, 0)
                    groups(pe, body)

                @block.scalar
                def _(act):
                    act.wait_ge(m_init, 1)

                    def body(g, s, i, last):
                        need(act, ct_st[s], 16 * i)
                        for j in range(G):
                            act.wait_ge(m_sum, g * G + j + 1)
                            nc.scalar.copy(ct[s][:, j, 0:MW], B[2 + j][:, 0:MW]).then_inc(m_ct, 1)
                        act.wait_ge(m_ct, G * (g + 1))
                        act.wait_ge(m_max, g + 1)
                        act.dma_start(tiles(CT, g), ct[s][:]).then_inc(ct_st[s], 16)
                    groups(act, body)
                    for s in range(2):
                        act.wait_ge(ct_st[s], 16 * PAIRS)

        ph = ExitStack()
        with ph:
            xin = [alloc(ph, f"n_x{s}", [P, G, D]) for s in range(2)]
            xpn = [alloc(ph, f"n_xp{s}", [P, G, D]) for s in range(2)]
            ssn = [alloc(ph, f"n_ss{s}", [P, G, 8]) for s in range(2)]
            cg = [alloc(ph, f"n_cg{s}", [P, G, CW]) for s in range(2)]
            we = [alloc(ph, f"n_weighted_edges{s}", [P, G, D]) for s in range(2)]
            wl = [alloc(ph, f"n_weighted_self{s}", [P, G, D]) for s in range(2)]
            il = [alloc(ph, f"n_last{s}", [P, G], i32) for s in range(2)]
            rows = [[B[4 * s + j][:, 0:D] for j in range(G)] for s in range(2)]
            x1 = [alloc(ph, f"n_x1{s}", [P, G, D]) for s in range(2)]
            xo = [alloc(ph, f"n_xo{s}", [P, G, D]) for s in range(2)]
            sf = [alloc(ph, f"n_self{s}", [P, G, HEADS]) for s in range(2)]
            mx = [alloc(ph, f"n_max{s}", [P, G, HEADS]) for s in range(2)]
            ea = [alloc(ph, f"n_exp{s}", [P, 2, G, HEADS]) for s in range(2)]
            den = [alloc(ph, f"n_den{s}", [P, G, HEADS]) for s in range(2)]
            st = [[alloc(ph, f"n_stats{k}{s}", [P, G, 6]) for s in range(2)] for k in range(2)]
            mv = [[alloc(ph, f"n_mv{k}{s}", [P, G, 2]) for s in range(2)] for k in range(2)]
            ve = [[alloc(ph, f"n_var{k}{s}", [P, G]) for s in range(2)] for k in range(2)]
            rs = [[alloc(ph, f"n_rstd{k}{s}", [P, G]) for s in range(2)] for k in range(2)]
            nm = [[alloc(ph, f"n_shift{k}{s}", [P, G]) for s in range(2)] for k in range(2)]
            half = alloc(ph, "n_half", [P, G])
            n_x, n_ld, n_cg = sems("n_x_loaded"), sems("n_loaded"), sems("n_gathered")
            x1_st, xo_st = sems("n_x1_stored"), sems("n_xo_stored")
            n_half, n_il, n_exl, n_exp, n_sc, n_y = (sem("n_half"), sem("n_il"), sem("n_exl"), sem("n_exp"),
                                                            sem("n_scaled"), sem("n_y"))
            n_var = [sem(f"n_var{k}") for k in range(2)]
            n_pow = [sem(f"n_pow{k}") for k in range(2)]
            n_nm = [sem(f"n_nm{k}") for k in range(2)]
            n_stat = [sem(f"n_stat{k}") for k in range(2)]
            n_x1, n_xo, n_ch = sem("n_x1"), sem("n_xo"), sem("n_chain")
            LOADS = 32
            with nc.Block() as block:
                @block.sync
                def _(sp):
                    def body(g, s, i, last):
                        need(sp, n_sc, 2 * (g - 1))
                        sp.dma_start(xpn[s][:], tiles(XP, g)).then_inc(n_ld[s], 16)
                        sp.dma_start(ssn[s][:], tiles(SS, g)).then_inc(n_ld[s], 16)
                        need(sp, n_y, G * (g - 1))
                        load_rows(sp, xin[s], x, g, last, n_x[s])
                    groups(sp, body)

                @block.gpsimd
                def _(pool):
                    nc.gpsimd.memset(half[:], -0.5).then_inc(n_half, 1)
                    pool.wait_ge(n_half, 1)

                    def gather(g, s):
                        need(pool, n_sc, 2 * (g - 1))
                        pool.sem_inc(turn, 1)
                        nc.gpsimd.tensor_copy(il[s][:], lastd[:, bass.ds(g * G, G)]).then_inc(n_il, 1)
                        pool.wait_ge(n_il, g + 1)
                        pool.sem_inc(turn, 1)
                        for j in range(G):
                            pool.indirect_dma_start(
                                out=cg[s][:, j, :], out_offset=None, in_=CT,
                                in_offset=bass.IndirectOffsetOnAxis(ap=il[s][:, j:j + 1], axis=0)).then_inc(n_cg[s], 16)

                    def power(k, g, s):
                        pool.wait_ge(n_var[k], g + 1)
                        need(pool, n_nm[k], g - 1)
                        nc.gpsimd.tensor_tensor(rs[k][s][:], ve[k][s][:], half[:], ALU.pow).then_inc(n_pow[k], 1)

                    for g in range(2):
                        gather(g, g % 2)

                    def body(g, s, i, last):
                        if not late(g, 2):
                            gather(g + 2, s)
                        power(0, g, s)
                        if not early(g, 1):
                            power(1, g - 1, 1 - s)
                    groups(pool, body)
                    power(1, GROUPS - 1, 1)

                @block.vector
                def _(dve):
                    c, STEPS = Count(dve, n_ch), 7
                    cs2 = [Count(dve, n_stat[k]) for k in range(2)]

                    def stats(k, g, s, rows):
                        cs2[k].at(g * 2)
                        for j in range(G):
                            if k == 0:
                                dve.wait_ge(n_y, g * G + j + 1)
                            o = nc.vector.bn_stats(st[k][s][:, j, :], rows[j])
                        cs2[k].step(o)
                        dve.sem_inc(dturn, 1)
                        for j in range(G):
                            o = nc.vector.bn_aggr(mv[k][s][:, j, :], st[k][s][:, j, :])
                        cs2[k].step(o)
                        nc.vector.tensor_scalar(ve[k][s][:], mv[k][s][:, :, 1], EPS, None, ALU.add).then_inc(n_var[k], 1)

                    def shift(k, g, s):
                        dve.wait_ge(n_pow[k], g + 1)
                        nc.vector.scalar_tensor_tensor(nm[k][s][:], mv[k][s][:, :, 0], -1.0, rs[k][s][:],
                                                       ALU.mult, ALU.mult).then_inc(n_nm[k], 1)

                    def exponents(g, s, i):
                        c.at(g * STEPS)
                        dve.wait_ge(n_ld[s], LOADS * (i + 1))
                        c.step(nc.vector.tensor_tensor(sf[s][:], ssn[s][:, :, 0:4], ssn[s][:, :, 4:8], ALU.add))
                        c.step(nc.vector.scalar_tensor_tensor(sf[s][:], sf[s][:], NEG_SLOPE, sf[s][:], ALU.mult, ALU.max))
                        dve.wait_ge(n_cg[s], 16 * G * (i + 1))
                        c.step(nc.vector.tensor_tensor(mx[s][:], sf[s][:], cg[s][:, :, MW:CW], ALU.max))
                        nc.vector.tensor_tensor(ea[s][:, 0], cg[s][:, :, MW:CW], mx[s][:], ALU.subtract)
                        nc.vector.tensor_tensor(ea[s][:, 1], sf[s][:], mx[s][:], ALU.subtract).then_inc(n_exl, 1)

                    def scale(g, s):
                        c.at(g * STEPS + 3)
                        dve.wait_ge(n_exp, g + 1)
                        c.step(nc.vector.tensor_tensor(den[s][:], cg[s][:, :, D:MW], ea[s][:, 0], ALU.mult))
                        c.step(nc.vector.scalar_tensor_tensor(den[s][:], den[s][:], 1e-12, ea[s][:, 1], ALU.add, ALU.add))
                        c.step(nc.vector.reciprocal(den[s][:], den[s][:]))
                        c.step(nc.vector.tensor_tensor(ea[s][:], ea[s][:], den[s][:].unsqueeze(1).to_broadcast(
                            [P, 2, G, HEADS]), ALU.mult))
                        assert c.n == STEPS - 3
                        need(dve, n_y, G * (g - 1))
                        for k, (w, a) in enumerate(((we[s][:], cg[s][:, :, 0:D]), (wl[s][:], xpn[s][:]))):
                            wh, ah = (b.rearrange("p t (h d) -> p t h d", h=HEADS) for b in (w, a))
                            nc.vector.tensor_tensor(wh, ah, ea[s][:, k].unsqueeze(3).to_broadcast([P, G, HEADS, HD]),
                                                    ALU.mult).then_inc(n_sc, 1)

                    def second(g, s):
                        dve.wait_ge(n_x1, g + 1)
                        stats(1, g, s, [x1[s][:, j, :] for j in range(G)])

                    def body(g, s, i, last):
                        stats(0, g, s, rows[s])
                        if not early(g, 1):
                            second(g - 1, 1 - s)
                        if not late(g, 2):
                            exponents(g + 2, s, i + 1)
                            scale(g + 2, s)
                        shift(0, g, s)
                        if not early(g, 1):
                            shift(1, g - 1, 1 - s)
                    for g in range(2):
                        exponents(g, g, 0)
                        scale(g, g)
                    groups(dve, body)
                    second(GROUPS - 1, 1)
                    shift(1, GROUPS - 1, 1)

                @block.tensor
                def _(pe):
                    def body(g, s, i, last):
                        pe.wait_ge(n_x[s], 16 * (i + 1) + 16 * last)
                        need(pe, n_x1, g - 1)
                        for j in range(G):
                            nc.tensor.matmul(rows[s][j], ident[:], xin[s][:, j, :], start=True, stop=False)
                            nc.tensor.matmul(rows[s][j], ones[0:1, :], biasb[0:1, :], start=False, stop=False)
                        pe.wait_ge(n_sc, 2 * (g + 1))
                        for j in range(G):
                            nc.tensor.matmul(rows[s][j], ident[:], we[s][:, j, :], start=False, stop=False)
                            nc.tensor.matmul(rows[s][j], ident[:], wl[s][:, j, :], start=False, stop=True)\
                                .then_inc(n_y, 1)
                    groups(pe, body)

                @block.scalar
                def _(act):
                    def first_norm(g, s, i):
                        need(act, x1_st[s], 16 * i)
                        act.wait_ge(n_nm[0], g + 1)
                        for j in range(G):
                            o = nc.scalar.activation(x1[s][:, j, :], rows[s][j], ACT.Identity,
                                                     bias=nm[0][s][:, j:j + 1], scale=rs[0][s][:, j:j + 1])
                        o.then_inc(n_x1, 1)
                        act.wait_ge(n_x1, g + 1)
                        act.dma_start(tiles(X1, g), x1[s][:]).then_inc(x1_st[s], 16)

                    def second_norm(g, s, i, last):
                        need(act, xo_st[s], 16 * i)
                        act.wait_ge(n_nm[1], g + 1)
                        for j in range(G):
                            o = nc.scalar.activation(xo[s][:, j, :], x1[s][:, j, :], ACT.Identity,
                                                     bias=nm[1][s][:, j:j + 1], scale=rs[1][s][:, j:j + 1])
                        o.then_inc(n_xo, 1)
                        act.wait_ge(n_xo, g + 1)
                        if not last:
                            act.dma_start(tiles(out, g), xo[s][:]).then_inc(xo_st[s], 16)
                            return
                        act.dma_start(tiles(out, g, TAIL_TILES), xo[s][:, 0:TAIL_TILES, :]).then_inc(xo_st[s], 16)
                        act.dma_start(out[N - TAIL_ROWS:N, :], xo[s][0:TAIL_ROWS, TAIL_TILES, :]).then_inc(xo_st[s], 16)

                    def exponentials(g, s):
                        act.wait_ge(n_exl, g + 1)
                        nc.scalar.activation(ea[s][:], ea[s][:], ACT.Exp).then_inc(n_exp, 1)

                    def body(g, s, i, last):
                        if not late(g, 2):
                            exponentials(g + 2, s)
                        first_norm(g, s, i)
                        if not early(g, 1):
                            second_norm(g - 1, 1 - s, i if s == 1 else i - 1, False)
                    for g in range(2):
                        exponentials(g, g)
                    groups(act, body)
                    second_norm(GROUPS - 1, 1, PAIRS - 1, True)
                    act.wait_ge(xo_st[0], 16 * PAIRS)
                    act.wait_ge(xo_st[1], 16 * PAIRS + 16)
                    for s in range(2):
                        act.wait_ge(x1_st[s], 16 * PAIRS)

        ph = ExitStack()
        with ph:
            es = [alloc(ph, f"es{s}", [P, G, 4], i32) for s in range(2)]
            nx = [alloc(ph, f"next{s}", [P, G, 1], i32) for s in range(2)]
            ag = [alloc(ph, f"ag{s}", [P, G, D]) for s in range(2)]
            bg = [alloc(ph, f"bg{s}", [P, G, D]) for s in range(2)]
            eg = [alloc(ph, f"eg{s}", [P, G, P]) for s in range(2)]
            ar = [alloc(ph, f"ar{s}", [P, G, D]) for s in range(2)]
            hT = [[alloc(ph, f"hT{s}{k}", [P, 4, G * P], f32r) for k in range(2)] for s in range(2)]
            eT = [[alloc(ph, f"u_eT{s}{k}", [P, G * P], f32r) for k in range(2)] for s in range(2)]
            h1 = [alloc(ph, f"h1{k}", [P, 3, G * P], f32r) for k in range(2)]
            h1t = alloc(ph, "h1t", [T0, G * P], f32r)
            h2 = [alloc(ph, f"h2{k}", [C1, 3, G * P], f32r) for k in range(2)]
            mg = [[alloc(ph, f"u_msg{s}{k}", [P, G, HW], f32r) for k in range(2)] for s in range(2)]
            th = [alloc(ph, f"tanh{k}", [P, G * P]) for k in range(2)]
            mf = [alloc(ph, f"message{k}", [P, D]) for k in range(2)]
            gs = [alloc(ph, f"gate{k}", [P, D]) for k in range(2)]
            cc = [alloc(ph, f"u_sum{s}", [P, G, HW]) for s in range(2)]
            kf = [alloc(ph, f"u_key{s}", [P, G]) for s in range(2)]
            nf = [alloc(ph, f"u_next{s}", [P, G]) for s in range(2)]
            km = [alloc(ph, f"u_key127{s}", [P, G + 1]) for s in range(2)]
            si = [alloc(ph, f"u_row{s}", [P, G], i32) for s in range(2)]
            sel = alloc(ph, "u_sel", [P, G, P], f32r)
            car = alloc(ph, "u_car", [P, G, P])
            rc = [alloc(ph, f"u_rc{s}", [P, G, 1]) for s in range(2)]
            y = [alloc(ph, f"u_y{s}", [P, G, D]) for s in range(2)]
            st = [alloc(ph, f"u_stats{s}", [P, G, 6]) for s in range(2)]
            mv = [alloc(ph, f"u_mv{s}", [P, G, 2]) for s in range(2)]
            ve = [alloc(ph, f"u_var{s}", [P, G]) for s in range(2)]
            rs = [alloc(ph, f"u_rstd{s}", [P, G]) for s in range(2)]
            nm = [alloc(ph, f"u_shift{s}", [P, G]) for s in range(2)]
            half = alloc(ph, "u_half", [P, G])
            es_ld, gath, o_st = sems("u_es_loaded"), sems("u_gathered"), sems("u_out_stored")
            u_half, u_keys, u_tp, u_td, u_ta = sem("u_half"), sem("u_keys"), sem("u_tp"), sem("u_td"), sem("u_ta")
            u_l, u_h, u_q, u_g, u_m = sem("u_l"), sem("u_h"), sem("u_q"), sem("u_g"), sem("u_m")
            u_kt, u_sel, u_sum, u_cc, u_ar = sem("u_kt"), sem("u_sel"), sem("u_sum"), sem("u_cc"), sem("u_ar")
            u_var, u_pow, u_nm, u_xo, u_si = sem("u_var"), sem("u_pow"), sem("u_nm"), sem("u_xo"), sem("u_si")
            u_init, u_chk, u_chf, u_chs, u_chn, u_y = (sem("u_init"), sem("u_chain_keys"), sem("u_chain_fin"),
                                                       sem("u_chain_sel"), sem("u_chain_row"), sem("u_y"))
            u_hl, u_mf, u_mh = sem("u_hl"), sem("u_mf"), sem("u_mh")
            JOBS = 5
            BL = (2, 3, 4)
            use_bank = [BL[0], BL[1], BL[2], BL[0], BL[1], BL[2], BL[0]]
            prev_use = [6 - 7, 4 - 7, 5 - 7, 0, 1, 2, 3]

            with nc.Block() as block:
                @block.sync
                def _(sp):
                    def load(g, s):
                        need(sp, u_keys, g - 1)
                        sp.dma_start(es[s][:], tiles(ES, g)).then_inc(es_ld[s], 16)
                        with nc.allow_non_contiguous_dma(reason="one key of each row"):
                            sp.dma_start(nx[s][:], shifted(ES, g, 1)[:, :, 0:1]).then_inc(es_ld[s], 16)
                    load(0, 0)
                    load(1, 1)

                    def body(g, s, i, last):
                        if not late(g, 2):
                            sp.wait_ge(gath[s], 48 * G * (i + 1))
                            load(g + 2, s)
                    groups(sp, body)

                @block.gpsimd
                def _(pool):
                    nc.gpsimd.memset(half[:], -0.5).then_inc(u_half, 1)
                    pool.wait_ge(u_half, 1)

                    def gather(g, s, i):
                        pool.wait_ge(es_ld[s], 32 * (i + 1))
                        need(pool, u_ar, g - 1)
                        for tables, job in ((((0, ag, X1), (1, bg, X1)), 4), (((2, eg, e128),), 5)):
                            need(pool, u_tp, JOBS * (g - 2) + job)
                            pool.sem_inc(turn, 1)
                            for j in range(G):
                                for k, buf, table in tables:
                                    pool.indirect_dma_start(
                                        out=buf[s][:, j, :], out_offset=None, in_=table,
                                        in_offset=bass.IndirectOffsetOnAxis(ap=es[s][:, j, k:k + 1], axis=0))\
                                        .then_inc(gath[s], 16)

                    def scatter(g, s):
                        pool.wait_ge(u_xo, g + 1)
                        pool.wait_ge(u_si, g + 1)
                        pool.sem_inc(turn, 1)
                        for j in range(G):
                            pool.indirect_dma_start(
                                out=out, out_offset=bass.IndirectOffsetOnAxis(ap=si[s][:, j:j + 1], axis=0),
                                in_=y[s][:, j, :], in_offset=None, bounds_check=N - 1, oob_is_err=False)\
                                .then_inc(o_st[s], 16)

                    def power(g, s):
                        pool.wait_ge(u_var, g + 1)
                        need(pool, u_nm, g - 1)
                        need(pool, u_xo, g - 1)
                        nc.gpsimd.tensor_tensor(rs[s][:], ve[s][:], half[:], ALU.pow).then_inc(u_pow, 1)
                    gather(0, 0, 0)
                    gather(1, 1, 0)

                    def body(g, s, i, last):
                        if not late(g, 2):
                            gather(g + 2, s, i + 1)
                        if not early(g, 2):
                            scatter(g - 2, s)
                        if not early(g, 1):
                            power(g - 1, 1 - s)
                    groups(pool, body)
                    scatter(GROUPS - 2, 0)
                    power(GROUPS - 1, 1)
                    scatter(GROUPS - 1, 1)
                    for s in range(2):
                        pool.wait_ge(o_st[s], 16 * G * PAIRS)

                @block.tensor
                def _(pe):
                    pe.wait_ge(u_init, 1)

                    def transposes(g, s, i, k):
                        if k == 0:
                            pe.wait_ge(gath[s], 48 * G * (i + 1))
                        need(pe, u_td, JOBS * g + (k - 1 if k >= 2 else (0, -1)[k]))
                        if k == 1:
                            need(pe, u_sel, g - 1)
                        for j in range(G):
                            a = (ag, ag, bg, bg)[k][s][:, j, (k % 2) * P:(k % 2) * P + P] if k < 4 else eg[s][:, j, :]
                            o = nc.tensor.transpose(B[k % 2][:, j * P:(j + 1) * P], a, ident[:])
                        o.then_inc(u_tp, 1)

                    def product(acc, terms, ready=None, stacked=None):
                        first, n = True, 3 * len(terms) + (stacked is not None)
                        for k, (a, b) in enumerate(terms):
                            if ready is not None:
                                pe.wait_ge(u_hl, ready + k)
                            for p, q in ((0, 0), (0, 1), (1, 0)):
                                n -= 1
                                o = nc.tensor.matmul(acc, a[p], b[q], start=first, stop=(n == 0))
                                first = False
                        if stacked is not None:
                            if ready is not None:
                                pe.wait_ge(u_hl, ready + len(terms))
                            o = nc.tensor.matmul(acc, stacked[0], stacked[1], start=False, stop=True)
                        return o

                    def combine(g, s, j):
                        t = g * G + j
                        need(pe, u_cc, t)
                        if j == 0:
                            pe.wait_ge(u_sel, g + 1)
                            pe.wait_ge(u_m, (g + 1) * G)
                        acc = B[7][:, 0:HW]
                        prev = cc[s][:, j - 1, :] if j else cc[1 - s][:, G - 1, :]
                        for k in range(2):
                            nc.tensor.matmul(acc, sel[:, j, :], mg[s][k][:, j, :], start=(k == 0), stop=False)
                        nc.tensor.matmul(acc, car[:, j, :], prev, start=False, stop=True).then_inc(u_sum, 1)

                    def body(g, s, i, last):
                        for m, (a, n) in enumerate(M0):
                            if m == 0:
                                pe.wait_ge(u_td, JOBS * (g + 1))
                            need(pe, u_h, 7 * g + prev_use[m] + 1)
                            w, rows_, cols = (w0r, n, slice(a, a + n)) if m < 3 else (w0t, T0, slice(0, T0))
                            o = product(B[use_bank[m]][0:rows_, :],
                                        [((w[0][:, k, cols], w[1][:, k, cols]), (hT[s][0][:, k, :], hT[s][1][:, k, :]))
                                         for k in range(4)])
                            o.then_inc(u_l, 1)
                            if not late(g, 1):
                                transposes(g + 1, 1 - s, i if s == 0 else i + 1, m)
                        for m, (a, n) in enumerate(M1):
                            need(pe, u_h, 7 * g + prev_use[4 + m] + 1)
                            o = product(B[use_bank[4 + m]][0:n, :],
                                        [((w1r[0][0:kn, k, a:a + n], w1r[1][0:kn, k, a:a + n]),
                                          (h1[0][0:kn, k, :], h1[1][0:kn, k, :])) for k, (_, kn) in enumerate(M0[:3])],
                                        ready=7 * g + 1 if m == 0 else None, stacked=(w1t[:, a:a + n], h1t[:]))
                            o.then_inc(u_l, 1)
                        if not late(g, 1):
                            transposes(g + 1, 1 - s, i if s == 0 else i + 1, 4)
                        for j in range(G):
                            if not early(g, 1):
                                combine(g - 1, 1 - s, j)
                            t = g * G + j
                            need(pe, u_mf, t - 1)
                            e = slice(j * P, (j + 1) * P)
                            rows_of = [kn + (k == 2) for k, (_, kn) in enumerate(M1)]
                            product(B[5 + j % 2][:, D:2 * D],
                                    [((eT[s][0][:, e], eT[s][1][:, e]), (wgr[0][:], wgr[1][:]))])
                            product(B[5 + j % 2][:, 0:D],
                                    [((h2[0][0:kn, k, e], h2[1][0:kn, k, e]), (w2r[0][0:kn, k, :], w2r[1][0:kn, k, :]))
                                     for k, kn in enumerate(rows_of)], ready=7 * g + 5 if j == 0 else None).then_inc(u_q, 1)
                        need(pe, u_td, JOBS * (g + 1 if late(g, 1) else g + 2))
                        pe.wait_ge(u_keys, g + 1)
                        for j in range(G):
                            o = nc.tensor.transpose(B[1][:, j * P:(j + 1) * P], kf[s][:, j:j + 1].to_broadcast([P, P]), ident[:])
                        o.then_inc(u_kt, 1)
                    for k in range(JOBS):
                        transposes(0, 0, 0, k)
                    groups(pe, body)
                    for j in range(G):
                        combine(GROUPS - 1, 1, j)

                @block.scalar
                def _(act):
                    def evac(g, s, k):
                        act.wait_ge(u_tp, JOBS * g + k + 1)
                        nc.scalar.copy(hT[s][0][:, k, :] if k < 4 else eT[s][0][:], B[k % 2][:]).then_inc(u_ta, 1)

                    def keep(g, s, i):
                        act.wait_ge(gath[s], 48 * G * (i + 1))
                        need(act, u_y, g - 1)
                        nc.scalar.copy(ar[s][:], ag[s][:]).then_inc(u_ar, 1)

                    def norm(g, s, i):
                        act.wait_ge(u_nm, g + 1)
                        need(act, o_st[s], 16 * G * i)
                        for j in range(G):
                            o = nc.scalar.activation(y[s][:, j, :], y[s][:, j, :], ACT.Identity,
                                                     bias=nm[s][:, j:j + 1], scale=rs[s][:, j:j + 1])
                        o.then_inc(u_xo, 1)

                    def high_message(g, s, j):
                        act.wait_ge(u_mf, g * G + j + 1)
                        need(act, u_sum, G * (g - 1))
                        nc.scalar.copy(mg[s][0][:, j, 0:D], mf[j % 2][:]).then_inc(u_mh, 1)

                    def hidden(use, b, acc, high, bias, n, again=0):
                        act.wait_ge(u_l, use + 1)
                        need(act, u_hl, use - 1 + again)
                        nc.scalar.activation(th[b][0:n, :], acc, ACT.Tanh, bias=bias)
                        nc.scalar.activation(high, acc, ACT.Tanh, bias=bias).then_inc(u_h, 1)

                    def body(g, s, i, last):
                        for m, (a, n) in enumerate(M0):
                            high, n = (h1[0][:, m, :], n) if m < 3 else (h1t[:], T0)
                            hidden(7 * g + m, m % 2, B[use_bank[m]][0:n, :], high, b0s[0:n, m:m + 1], n,
                                   again=(m == 0))
                            if not late(g, 1):
                                evac(g + 1, 1 - s, m)
                        for m, (a, n) in enumerate(M1):
                            hidden(7 * g + 4 + m, m % 2, B[use_bank[4 + m]][0:n, :], h2[0][0:n, m, :], b1s[0:n, m:m + 1], n)
                        if not late(g, 1):
                            evac(g + 1, 1 - s, 4)
                        for j in range(G):
                            t = g * G + j
                            act.wait_ge(u_q, t + 1)
                            need(act, u_mf, t - 1)
                            nc.scalar.copy(gs[j % 2][:], B[5 + j % 2][:, D:2 * D]).then_inc(u_g, 1)
                            if j:
                                high_message(g, s, j - 1)
                        high_message(g, s, G - 1)
                        if not early(g, 2):
                            norm(g - 2, s, i - 1)
                        if not late(g, 1):
                            keep(g + 1, 1 - s, i if s == 0 else i + 1)
                    act.wait_ge(u_init, 1)
                    for k in range(JOBS):
                        evac(0, 0, k)
                    keep(0, 0, 0)
                    groups(act, body)
                    norm(GROUPS - 2, 0, PAIRS - 1)
                    norm(GROUPS - 1, 1, PAIRS - 1)

                @block.vector
                def _(dve):
                    ck, cf, cs_, cn = Count(dve, u_chk), Count(dve, u_chf), Count(dve, u_chs), Count(dve, u_chn)
                    for s in range(2):
                        ck.did(nc.vector.memset(km[s][:], -1.0))
                        ck.did(nc.vector.memset(mg[s][0][:, :, D:D + 1].bitcast(f32), 1.0))
                        ck.did(nc.vector.memset(mg[s][0][:, :, D + 1:HW].bitcast(f32), 0.0))
                        ck.did(nc.vector.memset(mg[s][1][:, :, D:HW].bitcast(f32), 0.0))
                    ck.did(nc.vector.memset(h2[0][:, 2, :].bitcast(f32), 1.0))
                    ck.did(nc.vector.memset(h2[1][:, 2, :].bitcast(f32), 0.0))
                    nc.vector.memset(cc[1][:], 0.0).then_inc(u_init, 1)
                    ck.wait()
                    base0 = ck.n

                    def evac(g, s, k):
                        dve.wait_ge(u_ta, JOBS * g + k + 1)
                        hi, lo = (hT[s][q][:, k, :] if k < 4 else eT[s][q][:] for q in range(2))
                        nc.vector.tensor_tensor(lo, B[k % 2][:], hi.bitcast(f32), ALU.subtract).then_inc(u_td, 1)

                    def low_message(g, s, j):
                        dve.wait_ge(u_mh, g * G + j + 1)
                        nc.vector.tensor_tensor(mg[s][1][:, j, 0:D], mf[j % 2][:], mg[s][0][:, j, 0:D].bitcast(f32),
                                                ALU.subtract).then_inc(u_m, 1)

                    def low(use, h, m, n):
                        dve.wait_ge(u_h, use + 1)
                        if m == 3:
                            r = slice(STACK[2], T0)
                            nc.vector.tensor_tensor(h1t[r], th[1][r], h1t[r].bitcast(f32), ALU.subtract).then_inc(u_hl, 1)
                            return
                        nc.vector.tensor_tensor(h[1][0:n, m, :], th[m % 2][0:n, :], h[0][0:n, m, :].bitcast(f32),
                                                ALU.subtract).then_inc(u_hl, 1)

                    def keys(g, s, i):
                        ck.at(base0 + g * 2)
                        dve.wait_ge(es_ld[s], 32 * (i + 1))
                        ck.did(nc.vector.tensor_copy(nf[s][:], nx[s][:, :, 0]))
                        nc.vector.tensor_copy(kf[s][:], es[s][:, :, 0]).then_inc(u_keys, 1)
                        dve.wait_ge(u_keys, g + 1)
                        nc.vector.tensor_scalar(km[s][:, 1:G + 1], kf[s][:], is127[:, 0:1], is127[:, 1:2],
                                                ALU.mult, ALU.add)
                        ck.step(nc.vector.tensor_copy(km[s][:, 0:1], km[1 - s][:, G:G + 1]))

                    def row_index(g, s, i):
                        need(dve, o_st[s], 16 * G * i)
                        cn.at(g)
                        cn.step(nc.vector.tensor_tensor(nf[s][:], kf[s][:], nf[s][:], ALU.is_equal))
                        nc.vector.scalar_tensor_tensor(si[s][:], nf[s][:], OOB, kf[s][:], ALU.mult, ALU.add)\
                            .then_inc(u_si, 1)

                    def finish(g, s, i):
                        cf.at(g * 3)
                        cf.step(nc.vector.reciprocal(rc[s][:], cc[s][:, :, D:D + 1]))
                        need(dve, u_xo, g - 1)
                        dve.wait_ge(u_ar, g + 1)
                        for j in range(G):
                            o = nc.vector.scalar_tensor_tensor(y[s][:, j, :], cc[s][:, j, 0:D], rc[s][:, j, :],
                                                               ar[s][:, j, :], ALU.mult, ALU.add)
                        o.then_inc(u_y, 1)
                        dve.wait_ge(u_y, g + 1)
                        for j in range(G):
                            o = nc.vector.bn_stats(st[s][:, j, :], y[s][:, j, :])
                        cf.step(o)
                        dve.sem_inc(dturn, 1)
                        for j in range(G):
                            o = nc.vector.bn_aggr(mv[s][:, j, :], st[s][:, j, :])
                        cf.step(o)
                        nc.vector.tensor_scalar(ve[s][:], mv[s][:, :, 1], EPS, None, ALU.add).then_inc(u_var, 1)

                    def shift(g, s):
                        dve.wait_ge(u_pow, g + 1)
                        nc.vector.scalar_tensor_tensor(nm[s][:], mv[s][:, :, 0], -1.0, rs[s][:],
                                                       ALU.mult, ALU.mult).then_inc(u_nm, 1)

                    def sums(g, s, j):
                        dve.wait_ge(u_sum, g * G + j + 1)
                        nc.vector.tensor_copy(cc[s][:, j, :], B[7][:, 0:HW]).then_inc(u_cc, 1)
                        if j == G - 1:
                            dve.wait_ge(u_cc, (g + 1) * G)

                    def body(g, s, i, last):
                        for m, (a, n) in enumerate(M0):
                            low(7 * g + m, h1, m, n)
                            if not late(g, 1):
                                evac(g + 1, 1 - s, m)
                            if m == 1:
                                keys(g, s, i)
                        if not early(g, 2):
                            shift(g - 2, s)
                        for m, (a, n) in enumerate(M1):
                            low(7 * g + 4 + m, h2, m, n)
                        for j in range(G):
                            if not early(g, 1):
                                sums(g - 1, 1 - s, j)
                            if j == 1 and not late(g, 1):
                                evac(g + 1, 1 - s, 4)
                            dve.wait_ge(u_g, g * G + j + 1)
                            need(dve, u_m, g * G + j - 1)
                            nc.vector.tensor_tensor(mf[j % 2][:], B[5 + j % 2][:, 0:D], gs[j % 2][:],
                                                    ALU.mult).then_inc(u_mf, 1)
                            if j:
                                low_message(g, s, j - 1)
                        low_message(g, s, G - 1)
                        dve.wait_ge(u_kt, g + 1)
                        kb = B[1][:].rearrange("p (t n) -> p t n", t=G)
                        nc.vector.tensor_tensor(sel[:], kb, kf[s][:].unsqueeze(2).to_broadcast([P, G, P]), ALU.is_equal)
                        nc.vector.tensor_tensor(car[:], kb, km[s][:, 0:G].unsqueeze(2).to_broadcast([P, G, P]),
                                                ALU.is_equal).then_inc(u_sel, 1)
                        if not early(g, 1):
                            k = i if s == 1 else i - 1
                            row_index(g - 1, 1 - s, k)
                            finish(g - 1, 1 - s, k)
                    dve.wait_ge(u_init, 1)
                    for k in range(JOBS):
                        evac(0, 0, k)
                    groups(dve, body)
                    shift(GROUPS - 2, 0)
                    for j in range(G):
                        sums(GROUPS - 1, 1, j)
                    row_index(GROUPS - 1, 1, PAIRS - 1)
                    finish(GROUPS - 1, 1, PAIRS - 1)
                    shift(GROUPS - 1, 1)

_INS = ['x', 'src', 'dst', 'edge_attr_128', 'edge_attr_32', 'L0_gnn_lin_W', 'L0_gnn_att_src', 'L0_gnn_att_dst',
        'L0_gnn_lin_edge_W', 'L0_gnn_att_edge', 'L0_gnn_bias', 'L1_gnn_W0', 'L1_gnn_b0', 'L1_gnn_W1',
        'L1_gnn_b1', 'L1_gnn_W2', 'L1_gnn_b2', 'L1_gnn_Wg']


def kernel(**inputs):
    import concourse.bacc as bacc
    import numpy as np
    from concourse.bass_utils import run_bass_kernel_spmd

    nc = bacc.Bacc("TRN2", target_bir_lowering=False, num_devices=1)
    arrays, args = {}, []
    for name in _INS:
        a = np.ascontiguousarray(inputs[name])
        arrays[f"in_{name}"] = a
        args.append(nc.dram_tensor(f"in_{name}", a.shape, mybir.dt.from_np(a.dtype), kind="ExternalInput").ap())
    shape = tuple(inputs['x'].shape)
    args.append(nc.dram_tensor("out_x", shape, mybir.dt.float32, kind="ExternalOutput").ap())
    gnn_kernel(nc, *args)
    r = run_bass_kernel_spmd(nc, [arrays], core_ids=[0])
    return r.results[0]["out_x"]
```
